# Optimizing a Trainium2 kernel written in Bass

```python
import numpy as np
import jax
import jax.numpy as jnp

def _softmax(x, axis=-1):
    return jax.nn.softmax(x, axis=axis)

def _gelu(x):
    return jax.nn.gelu(x, approximate=True)

def _silu(x):
    return jax.nn.silu(x)

def _sigmoid(x):
    return jax.nn.sigmoid(x)

def _layernorm(x, axis=-1, eps=1e-05):
    m = jnp.mean(x, axis=axis, keepdims=True)
    v = jnp.var(x, axis=axis, keepdims=True)
    return (x - m) / jnp.sqrt(v + eps)

def _scatter_add(tgt, idx, src, axis=0):
    return tgt.at[idx].add(src)

def _segment_sum(src, seg, n):
    return jax.ops.segment_sum(src, seg, n)
kernel_name = 'mk_prb_d1_jaxref_r8_7f3f34'

def setup_inputs(seed: int=0):
    np.random.seed(seed)
    _w = jnp.asarray

    def _L0_attn_setup():
        import jax, jax.numpy as jnp
        import numpy as np
        D_MODEL = 128
        N_HEADS = 16
        N_GROUPS = 4
        D_K = D_MODEL // N_HEADS
        HEADS_PER_GROUP = N_HEADS // N_GROUPS

        def rope(x):
            s, d = (x.shape[1], x.shape[2])
            theta = 1.0 / 10000.0 ** (jnp.arange(d // 2, dtype=jnp.float32) / (d // 2))
            ang = jnp.arange(s, dtype=jnp.float32)[:, None] * theta[None, :]
            cos, sin = (jnp.cos(ang), jnp.sin(ang))
            xe, xo = (x[..., 0::2], x[..., 1::2])
            return jnp.concatenate([xe * cos - xo * sin, xe * sin + xo * cos], axis=-1)
        key = jax.random.key(seed)
        k1, k2, k3, k4, k5 = jax.random.split(key, 5)
        b, s = (1, 256)
        scale = 0.02
        X = jax.random.normal(k1, (b, s, D_MODEL), dtype=jnp.float32)
        W_q = jax.random.normal(k2, (D_MODEL, D_MODEL), dtype=jnp.float32) * scale
        W_k = jax.random.normal(k3, (N_GROUPS * D_K, D_MODEL), dtype=jnp.float32) * scale
        W_v = jax.random.normal(k4, (N_GROUPS * D_K, D_MODEL), dtype=jnp.float32) * scale
        W_o = jax.random.normal(k5, (D_MODEL, D_MODEL), dtype=jnp.float32) * scale
        return {'X': X, 'W_q': W_q, 'W_k': W_k, 'W_v': W_v, 'W_o': W_o}
    _L0_attn_in = _L0_attn_setup()

    def _L0_ffn_setup():
        import jax, jax.numpy as jnp
        import numpy as np
        B, S, D, F, E = (1, 128, 128, 512, 8)
        EPS = 1e-05

        def _sublayer(xs, g, b, W1e, b1e, W2e, b2e):
            mu = jnp.mean(xs, axis=-1, keepdims=True)
            var = jnp.mean(jnp.square(xs - mu), axis=-1, keepdims=True)
            h = (xs - mu) * jax.lax.rsqrt(var + EPS) * g + b
            return xs + jax.nn.relu(h @ W1e.T + b1e) @ W2e.T + b2e
        key = jax.random.key(seed)
        ks = jax.random.split(key, 4)
        x = jax.random.normal(ks[0], (B, S, D), jnp.float32)
        centroids = jax.random.normal(ks[1], (E, D), jnp.float32) * 0.1
        gamma = jnp.ones((E, D), jnp.float32)
        beta = jnp.zeros((E, D), jnp.float32)
        W1 = jax.random.normal(ks[2], (E, F, D), jnp.float32) * 0.02
        b1 = jnp.zeros((E, F), jnp.float32)
        W2 = jax.random.normal(ks[3], (E, D, F), jnp.float32) * 0.02
        b2 = jnp.zeros((E, D), jnp.float32)
        return {'x': x, 'centroids': centroids, 'gamma': gamma, 'beta': beta, 'W1': W1, 'b1': b1, 'W2': W2, 'b2': b2}
    _L0_ffn_in = _L0_ffn_setup()
    _d = {'L0_attn_X': _L0_attn_in['X'], 'L0_attn_W_q': _L0_attn_in['W_q'], 'L0_attn_W_k': _L0_attn_in['W_k'], 'L0_attn_W_v': _L0_attn_in['W_v'], 'L0_attn_W_o': _L0_attn_in['W_o'], 'L0_ffn_centroids': _L0_ffn_in['centroids'], 'L0_ffn_gamma': _L0_ffn_in['gamma'], 'L0_ffn_beta': _L0_ffn_in['beta'], 'L0_ffn_W1': _L0_ffn_in['W1'], 'L0_ffn_b1': _L0_ffn_in['b1'], 'L0_ffn_W2': _L0_ffn_in['W2'], 'L0_ffn_b2': _L0_ffn_in['b2']}
    _x0 = _d['L0_attn_X']
    _d['L0_attn_X'] = jax.random.normal(jax.random.fold_in(jax.random.key(seed), 1), (8, 512, 128), dtype=_x0.dtype)
    del _x0
    return _d

def reference(L0_attn_X, L0_attn_W_q, L0_attn_W_k, L0_attn_W_v, L0_attn_W_o, L0_ffn_centroids, L0_ffn_gamma, L0_ffn_beta, L0_ffn_W1, L0_ffn_b1, L0_ffn_W2, L0_ffn_b2):

    def _L0_attn_ref(X, W_q, W_k, W_v, W_o):
        import jax, jax.numpy as jnp
        import numpy as np
        D_MODEL = 128
        N_HEADS = 16
        N_GROUPS = 4
        D_K = D_MODEL // N_HEADS
        HEADS_PER_GROUP = N_HEADS // N_GROUPS

        def rope(x):
            s, d = (x.shape[1], x.shape[2])
            theta = 1.0 / 10000.0 ** (jnp.arange(d // 2, dtype=jnp.float32) / (d // 2))
            ang = jnp.arange(s, dtype=jnp.float32)[:, None] * theta[None, :]
            cos, sin = (jnp.cos(ang), jnp.sin(ang))
            xe, xo = (x[..., 0::2], x[..., 1::2])
            return jnp.concatenate([xe * cos - xo * sin, xe * sin + xo * cos], axis=-1)
        b, s, _ = X.shape
        Xr = rope(X)
        Q = (Xr @ W_q.T).reshape(b, s, N_HEADS, D_K).transpose(0, 2, 1, 3)
        K = (Xr @ W_k.T).reshape(b, s, N_GROUPS, D_K).transpose(0, 2, 1, 3)
        V = (Xr @ W_v.T).reshape(b, s, N_GROUPS, D_K).transpose(0, 2, 1, 3)
        Q = Q.reshape(b, N_GROUPS, HEADS_PER_GROUP, s, D_K)
        scores = jnp.einsum('bghsd,bgtd->bghst', Q, K) / jnp.sqrt(jnp.float32(D_K))
        mask = jnp.triu(jnp.ones((s, s), dtype=scores.dtype), k=1) * -1000000000.0
        attn = jax.nn.softmax(scores + mask, axis=-1)
        out = jnp.einsum('bghst,bgtd->bghsd', attn, V)
        out = out.reshape(b, N_HEADS, s, D_K).transpose(0, 2, 1, 3).reshape(b, s, D_MODEL)
        return out @ W_o.T

    def _L0_ffn_ref(x, centroids, gamma, beta, W1, b1, W2, b2):
        import jax, jax.numpy as jnp
        import numpy as np
        B, S, D, F, E = (1, 128, 128, 512, 8)
        EPS = 1e-05

        def _sublayer(xs, g, b, W1e, b1e, W2e, b2e):
            mu = jnp.mean(xs, axis=-1, keepdims=True)
            var = jnp.mean(jnp.square(xs - mu), axis=-1, keepdims=True)
            h = (xs - mu) * jax.lax.rsqrt(var + EPS) * g + b
            return xs + jax.nn.relu(h @ W1e.T + b1e) @ W2e.T + b2e
        feats = x.reshape(-1, x.shape[-1])
        scores = jax.lax.stop_gradient(feats @ centroids.T)
        expert = jnp.argmax(scores, axis=1)
        onehot = jax.nn.one_hot(expert, E, dtype=feats.dtype)
        alpha = jax.nn.sigmoid(jnp.sum(feats * centroids[expert], axis=-1, keepdims=True))
        ys = jax.vmap(_sublayer, in_axes=(None, 0, 0, 0, 0, 0, 0))(feats, gamma, beta, W1, b1, W2, b2)
        y = jnp.einsum('te,etd->td', onehot, ys)
        out = alpha * y + (1.0 - alpha) * feats
        return out.reshape(x.shape)
    x = L0_attn_X
    xn = _layernorm(x, axis=-1)
    x = x + _L0_attn_ref(xn, L0_attn_W_q, L0_attn_W_k, L0_attn_W_v, L0_attn_W_o) + _L0_ffn_ref(xn, L0_ffn_centroids, L0_ffn_gamma, L0_ffn_beta, L0_ffn_W1, L0_ffn_b1, L0_ffn_W2, L0_ffn_b2)
    return x

_drawn_inputs = setup_inputs


def setup_inputs(seed=0):
    import zlib

    import numpy as np

    out = dict(_drawn_inputs(seed))
    spreads = {'L0_ffn_gamma': (1.0, 0.6),
     'L0_ffn_beta': (0.0, 2.0),
     'L0_ffn_b1': (0.0, 0.618),
     'L0_ffn_b2': (0.0, 0.1)}
    factors = {'L0_attn_W_q': 8.0, 'L0_attn_W_k': 8.0, 'L0_attn_W_v': 8.0, 'L0_attn_W_o': 8.0}
    for name, (base, spread) in spreads.items():
        noise = np.random.default_rng([zlib.crc32(name.encode()), seed]).standard_normal(out[name].shape)
        drawn = base * np.exp(spread * noise) if base else spread * noise
        out[name] = jnp.asarray(drawn.astype(out[name].dtype))
    for name, factor in factors.items():
        out[name] = (out[name] * factor).astype(out[name].dtype)
    return out
```

```python
from contextlib import ExitStack

import numpy as np

import concourse.bass as bass
from concourse import mybir

F32 = mybir.dt.float32
BF16 = mybir.dt.bfloat16
I32 = mybir.dt.int32
ALU = mybir.AluOpType
ACT = mybir.ActivationFunctionType
AX = mybir.AxisListType.X

P = 128
NB = 8
NI = 4
NK = NB * NI
S = 512
D = 128
NH = 16
NG = 4
E = 8
F = 512
EPS = 1e-5
SCALE = 1.0 / float(np.sqrt(np.float32(8)))
NT = (NK * P + E * (P - 1)) // P
ROW = 1168
C_W1, C_W2, C_G, C_B, C_B1, C_B2 = 0, 512, 1024, 1025, 1026, 1040
K_ID, K_MASK, K_TRI, K_ONE, K_COS, K_SIN = 0, 128, 256, 384, 512, 768
K_IE, K_IE8, K_J, K_T, K_P, K_Z = 1024, 1032, 1040, 1072, 1112, 1113
KW = 1145
SPLIT = [(a, c) for a in range(3) for c in range(3)]
MROW = 96


class Flow:

    ENGINES = ("sync", "gpsimd", "scalar", "tensor", "vector")

    def __init__(self, nc, ctx):
        self.nc, self.ctx = nc, ctx
        self.queue = {e: [] for e in self.ENGINES}
        self.count, self.sems = {}, {}
        self.waited = {e: {} for e in self.ENGINES}

    def mark(self, sem, step):
        if sem not in self.sems:
            self.sems[sem] = self.ctx.enter_context(self.nc.semaphore(sem))
            self.count[sem] = 0
        self.count[sem] += step
        return sem, self.count[sem]

    def wait(self, eng, after):
        for m in after:
            if m is not None and self.waited[eng].get(m[0], 0) < m[1]:
                self.waited[eng][m[0]] = m[1]
                self.queue[eng].append(lambda e, s=self.sems[m[0]], v=m[1]: e.wait_ge(s, v))

    def do(self, eng, fn, after=(), sem=None, step=1):
        self.wait(eng, after)
        if sem is None:
            self.queue[eng].append(fn)
            return None
        m = self.mark(sem, step)
        self.queue[eng].append(lambda e, s=self.sems[sem]: fn(e).then_inc(s, step))
        return m

    def dma(self, eng, fn, after=(), sem=None):
        return self.do(eng, fn, after, sem, 16)

    def run(self, block):
        for name in self.ENGINES:
            def body(e, q=self.queue[name]):
                for f in q:
                    f(e)
            (block.sync if name == "sync" else block.gpsimd if name == "gpsimd" else block.scalar if name == "scalar"
             else block.tensor if name == "tensor" else block.vector)(body)


def build(nc, X_d, wq_d, wkv_d, wo_d, cen_d, tab_d, cst_d, out_d):
    with ExitStack() as ctx:
        fl = Flow(nc, ctx)
        do, dma = fl.do, fl.dma

        def sb(name, shape, dt=F32):
            return ctx.enter_context(nc.sbuf_tensor(name, shape, dt))

        def ps(name, shape, dt=F32):
            return ctx.enter_context(nc.psum_tensor(name, shape, dt))

        def dram(name, shape, dt=F32):
            return nc.dram_tensor(name, shape, dt, kind="Internal").ap()

        xs_d = dram("xs_d", (NT * P, D))
        ys_d = dram("ys_d", (NT * P, D))
        qd = [dram(f"qd{b}", (P, 3, S), BF16) for b in range(NB)]
        kd = [dram(f"kd{b}", (32, 3, S), BF16) for b in range(NB)]

        cst = sb("cst", [P, KW])
        idf = cst[:, K_ID:K_ID + P]
        idb = sb("idb", [P, P], BF16)
        maskb = sb("maskb", [P, P], BF16)
        trib = sb("trib", [P, P], BF16)
        oneb = sb("oneb", [P, P], BF16)
        cosT = cst[:, K_COS:K_COS + 256].rearrange("p (i c) -> p i c", i=NI)
        sinT = cst[:, K_SIN:K_SIN + 256].rearrange("p (i c) -> p i c", i=NI)
        wq = sb("wq", [P, P])
        wkv = sb("wkv", [P, 64])
        wo = sb("wo", [P, P])
        cen = sb("cen", [P, E])
        X = sb("X", [P, NK, D])
        xn = sb("xn", [P, 2, NI, D])
        xh = sb("xh", [P, NK, D])
        xr = sb("xr", [P, 2, NI, D])
        rt = sb("rt", [P, 2, NI, 64])
        xnT = sb("xnT", [P, S])
        xrT = sb("xrT", [P, S])
        qp = sb("qp", [P, 2, 3, S], BF16)
        kp = sb("kp", [32, 2, 3, S], BF16)
        qr = sb("qr", [P, S])
        kr = sb("kr", [32, S])
        Qop = sb("Qop", [P, 2, NH, S], BF16)
        Kop = sb("Kop", [P, 2, NG, S], BF16)
        V = sb("V", [P, NK, NG, 32])
        PT = [sb(f"PT{i}", [P, 4 * 1280]) for i in range(2)]
        st1, st2 = sb("st1", [P, NK, 6]), sb("st2", [P, NK, 6])
        mv1, mv2 = sb("mv1", [P, NK, 2]), sb("mv2", [P, NK, 2])
        rs1, rs2 = sb("rs1", [P, NK]), sb("rs2", [P, NK])
        mx = sb("mx", [P, 2, NI, 4])
        nm = sb("nm", [P, 2, NI, 2, 4], BF16)
        mT = sb("mT", [8, 2, S], BF16)
        O = sb("O", [P, 2, S])
        rden = sb("rden", [P, 2, NI, 4])
        att = sb("att", [P, 2, NI, D])
        attT = sb("attT", [P, S])
        wt = [sb(f"wt{i}", [P, ROW]) for i in range(2)]
        xt = [sb(f"xt{i}", [P, D]) for i in range(2)]
        hT = sb("hT", [P, 2, P])
        h1 = sb("h1", [P, 2, 4, P])
        yt = sb("yt", [P, 2, D])
        sc = sb("sc", [P, NK, E])
        smx, sam, alpha, ea = (sb(n, [P, NK]) for n in ("smx", "sam", "alpha", "ea"))
        eq, oh, tot, incl = (sb(n, [P, NK, E]) for n in ("eq", "oh", "tot", "incl"))
        ohb = sb("ohb", [P, NK, E], BF16)
        cmpn = sb("cmpn", [P, E, 32])
        ntl, tend, tst = (sb(n, [P, E]) for n in ("ntl", "tend", "tst"))
        cmpt = sb("cmpt", [P, NT, E])
        et = sb("et", [P, NT])
        posf = sb("posf", [P, NK])
        posi = sb("posi", [P, NK], I32)
        widx = sb("widx", [P, NT], I32)

        MX = [ps(f"MX{i}", [P, 512]) for i in range(2)]
        SC = [ps(f"SC{i}", [P, 512]) for i in range(2)]
        PV = ps("PV", [P, 512])
        MI = [ps(f"MI{i}", [P, 512]) for i in range(3)]

        mi_n = [0]
        mi_free = [[], [], []]

        def misc():
            k = mi_n[0] % 3
            mi_n[0] += 1
            return k

        l_c = dma("sync", lambda e: e.dma_start(cst[:, :], cst_d), sem="l_cst")
        x_in = []
        for b in range(NB):
            x_in.append(dma("sync", lambda e, b=b: e.dma_start(
                X[:, NI * b:NI * b + NI, :], X_d[b].rearrange("(i p) d -> p i d", p=P)), sem=f"l_x{b}"))
            if b == 0:
                for t, s in ((cen, cen_d), (wq, wq_d), (wkv, wkv_d), (wo, wo_d)):
                    l_w = dma("sync", lambda e, t=t, s=s: e.dma_start(t[:, :], s), sem="l_w")
        consts = None
        for t, k in ((idb, K_ID), (maskb, K_MASK), (trib, K_TRI), (oneb, K_ONE)):
            consts = do("scalar", lambda e, t=t, k=k: e.activation(t[:, :], cst[:, k:k + P], ACT.Copy),
                        [l_c], "consts")
        do("gpsimd", lambda e: e.memset(xt[0][:, :], 0.0), sem="clr")
        z_x = do("gpsimd", lambda e: e.memset(Kop[:, :, :, :].bitcast(F32), 0.0), sem="clr")
        do("gpsimd", lambda e: e.memset(Qop[:, 0, :, :].bitcast(F32), 0.0), sem="clr")
        z_o = do("gpsimd", lambda e: e.memset(Qop[:, 1, :, :].bitcast(F32), 0.0), sem="clr")
        z_k = do("vector", lambda e: e.memset(Kop[MROW:MROW + 2, :, :, :], 1.0), [z_o], "v_one")
        z_v = do("gpsimd", lambda e: e.memset(V[:, :, :, :], 1.0), sem="clr")
        zero_x = dma("sync", lambda e: e.dma_start(
            xs_d.rearrange("(t p) d -> p t d", p=P), xt[0][:, :].unsqueeze(1).to_broadcast([P, NT, D])),
            [z_x], "zx")

        st = {}

        def rstd(rs, mv, k0, after):
            r = rs[:, k0:k0 + NI]
            a = do("vector", lambda e: e.tensor_scalar(r, mv[:, k0:k0 + NI, 1], EPS, None, ALU.add), [after], "v_ln")
            a = do("scalar", lambda e: e.activation(r, r, ACT.Sqrt), [a], "a_ln")
            return do("vector", lambda e: e.reciprocal(r, r), [a], "v_ln")

        def norm(b):
            k0, u = NI * b, b % 2
            ks = range(k0, k0 + NI)
            for k in ks:
                a = do("vector", lambda e, k=k: e.bn_stats(st1[:, k, :], X[:, k, :]), [x_in[b]], "v_ln")
            for k in ks:
                a2 = do("vector", lambda e, k=k: e.bn_aggr(mv1[:, k, :], st1[:, k, :]), [a], "v_ln")
            a = rstd(rs1, mv1, k0, a2)
            for k in ks:
                a2 = do("vector", lambda e, k=k: e.tensor_scalar(
                    xn[:, u, k - k0, :], X[:, k, :], mv1[:, k, 0:1], rs1[:, k:k + 1], ALU.subtract, ALU.mult),
                    [a] + st.get(("xn", u), []), "v_ln")
            st["n", b] = a2
            for k in ks:
                a = do("vector", lambda e, k=k: e.bn_stats(st2[:, k, :], xn[:, u, k - k0, :]), [a2], "v_ln")
            for k in ks:
                a2 = do("vector", lambda e, k=k: e.bn_aggr(mv2[:, k, :], st2[:, k, :]), [a], "v_ln")
            a = rstd(rs2, mv2, k0, a2)
            for k in ks:
                st["h", b] = do("gpsimd", lambda e, k=k: e.tensor_scalar(
                    xh[:, k, :], xn[:, u, k - k0, :], mv2[:, k, 0:1], rs2[:, k:k + 1], ALU.subtract, ALU.mult),
                    [a], "g_xh")
            st["xs", b] = do("gpsimd", lambda e: e.tensor_tensor(
                X[:, k0:k0 + NI, :], X[:, k0:k0 + NI, :], xn[:, u, :, :], ALU.add), [st["n", b]], "g_xs")
            m = misc()
            for i in range(NI):
                t = do("tensor", lambda e, i=i: e.transpose(MI[m][:, i * P:i * P + P], xn[:, u, i, :], idf),
                       [l_c, st["n", b]] + mi_free[m], "p_xnT")
            c = do("scalar", lambda e: e.activation(xnT[:, :], MI[m][:, :], ACT.Copy),
                   [t, st.get("xnT")], "a_xnT")
            mi_free[m] = [c]
            m2 = misc()
            for i in range(NI):
                t = do("tensor", lambda e, i=i: e.matmul(MI[m2][:, i * E:i * E + E], xnT[:, i * P:i * P + P],
                                                         cen[:, :], start=True, stop=True),
                       [c, l_w] + mi_free[m2], "p_sc")
            st["xnT"] = t
            r = do("vector", lambda e: e.tensor_copy(
                sc[:, k0:k0 + NI, :], MI[m2][:, 0:NI * E].rearrange("p (i c) -> p i c", i=NI)), [t], "v_sc")
            mi_free[m2] = [r]
            st["sc"] = r

        def rope(b, eng):
            u = b % 2
            v = xn[:, u, :, :].rearrange("p i (c two) -> p i c two", two=2)
            xe, xo = v[:, :, :, 0], v[:, :, :, 1]
            lo, hi = xr[:, u, :, 0:64], xr[:, u, :, 64:128]
            sem = "v_rope" if eng == "vector" else "g_rope"
            w = [st["n", b], l_c] + st.get(("xr", u), [])
            do(eng, lambda e: e.tensor_tensor(lo, xe, cosT, ALU.mult), w, sem)
            a = do(eng, lambda e: e.tensor_tensor(rt[:, u, :, :], xo, sinT, ALU.mult), w, sem)
            a = do(eng, lambda e: e.tensor_tensor(lo, lo, rt[:, u, :, :], ALU.subtract), [a], sem)
            do(eng, lambda e: e.tensor_tensor(hi, xe, sinT, ALU.mult), sem=sem)
            a = do(eng, lambda e: e.tensor_tensor(rt[:, u, :, :], xo, cosT, ALU.mult), [a], sem)
            a = do(eng, lambda e: e.tensor_tensor(hi, hi, rt[:, u, :, :], ALU.add), [a], sem)
            st["r", b] = a
            st["xn", u] = [a, st["h", b], st["xs", b]]

        def project(b):
            u, k0 = b % 2, NI * b
            m = misc()
            for i in range(NI):
                t = do("tensor", lambda e, i=i: e.transpose(MI[m][:, i * P:i * P + P], xr[:, u, i, :], idf),
                       [l_c, st["r", b]] + mi_free[m], "p_xrT")
            st["xr", u] = [t]
            c = do("scalar", lambda e: e.activation(xrT[:, :], MI[m][:, :], ACT.Copy),
                   [t, st.get("xrT")], "a_xrT")
            mi_free[m] = [c]
            mq, mk, mv = misc(), misc(), misc()
            tq = do("tensor", lambda e: e.matmul(MI[mq][:, :], wq[:, :], xrT[:, :], start=True, stop=True),
                    [c, l_w] + mi_free[mq], "p_q")
            tk = do("tensor", lambda e: e.matmul(MI[mk][0:32, :], wkv[:, 0:32], xrT[:, :], start=True, stop=True),
                    mi_free[mk], "p_q")
            for i in range(NI):
                tv = do("tensor", lambda e, i=i: e.matmul(MI[mv][:, i * 32:i * 32 + 32], xrT[:, i * P:i * P + P],
                                                          wkv[:, 32:64], start=True, stop=True), mi_free[mv], "p_q")
            st["xrT"] = tv
            ends = []
            for t, src, part, rem, n, key in ((tq, MI[mq], qp, qr, P, "q"), (tk, MI[mk], kp, kr, 32, "k")):
                w = [t, st.get((key, u))]
                a = do("scalar", lambda e, part=part, src=src, n=n: e.activation(
                    part[0:n, u, 0, :], src[0:n, :], ACT.Copy), w, "a_sp")
                v = do("vector", lambda e, part=part, src=src, n=n, rem=rem: e.tensor_tensor(
                    rem[0:n, :], src[0:n, :], part[0:n, u, 0, :], ALU.subtract), [a, st.get((key, "r"))], "v_sp")
                ends.append(v)
                a = do("scalar", lambda e, part=part, n=n, rem=rem: e.activation(
                    part[0:n, u, 1, :], rem[0:n, :], ACT.Copy), [v], "a_sp")
                v = do("vector", lambda e, part=part, n=n, rem=rem: e.tensor_tensor(
                    part[0:n, u, 2, :], rem[0:n, :], part[0:n, u, 1, :], ALU.subtract), [a], "v_sp")
                st[key, "r"] = v
                dst = qd[b] if key == "q" else kd[b]
                st[key, u] = dma("sync", lambda e, part=part, n=n, dst=dst: e.dma_start(dst, part[0:n, u, :, :]),
                                 [v], f"st_{key}{u}")
            mi_free[mq], mi_free[mk] = [ends[0]], [ends[1]]
            st["V", b] = do("vector", lambda e: e.tensor_copy(
                V[:, k0:k0 + NI, :, 0:8], MI[mv][:, 0:P].rearrange("p (i g d) -> p i g d", i=NI, g=NG)),
                [tv, z_v], "v_v")
            mi_free[mv] = [st["V", b]]

        def operands(b):
            u = b % 2
            free = [z_k] + [st.get(("scored", b - 2, g)) for g in range(NG)]
            for r, (a, c) in enumerate(SPLIT):
                dma("sync", lambda e, r=r, a=a: e.dma_start(
                    Qop[8 * r:8 * r + 8, u, :, :], qd[b][:, a, :].rearrange("(h d) t -> d h t", d=8)),
                    [st["q", u]] + free, f"ld_op{u}")
                st["op", b] = dma("sync", lambda e, r=r, c=c: e.dma_start(
                    Kop[8 * r:8 * r + 8, u, :, :], kd[b][:, c, :].rearrange("(g d) t -> d g t", d=8)),
                    [st["k", u]], f"ld_op{u}")

        def route():
            seq = lambda fn, after=(), eng="vector": do(eng, fn, list(after), "v_rt")
            bc = lambda a: a.unsqueeze(2).to_broadcast([P, NK, E])
            kc = lambda o, n: cst[:, o:o + n]
            a = seq(lambda e: e.tensor_reduce(smx[:, :], sc[:, :, :], AX, ALU.max), [st["sc"], l_c])
            x = do("scalar", lambda e: e.activation(ea[:, :], smx[:, :], ACT.Exp, scale=-1.0), [a], "a_al")
            a = seq(lambda e: e.tensor_tensor(eq[:, :, :], sc[:, :, :], bc(smx[:, :]), ALU.is_equal), [a])
            a = seq(lambda e: e.scalar_tensor_tensor(
                out=eq[:, :, :], in0=eq[:, :, :], scalar=-8.0,
                in1=kc(K_IE8, E).unsqueeze(1).to_broadcast([P, NK, E]), op0=ALU.mult, op1=ALU.add), [a])
            a = seq(lambda e: e.tensor_reduce(sam[:, :], eq[:, :, :], AX, ALU.min), [a])
            a = seq(lambda e: e.tensor_tensor(oh[:, :, :], kc(K_IE, E).unsqueeze(1).to_broadcast([P, NK, E]),
                                              bc(sam[:, :]), ALU.is_equal), [a])
            a = seq(lambda e: e.tensor_copy(ohb[:, :, :], oh[:, :, :]), [a])
            m = misc()
            flat = ohb[:, :, :].rearrange("p k c -> p (k c)")
            do("tensor", lambda e: e.matmul(MI[m][:, 0:256], trib[:, :], flat, start=True, stop=True),
               [a, consts] + mi_free[m], "p_rt")
            t = do("tensor", lambda e: e.matmul(MI[m][:, 256:512], oneb[:, :], flat, start=True, stop=True),
                   sem="p_rt")
            a = seq(lambda e: e.tensor_scalar(ea[:, :], ea[:, :], 1.0, None, ALU.add), [x])
            st["alpha"] = seq(lambda e: e.reciprocal(alpha[:, :], ea[:, :]), [a])
            a = seq(lambda e: e.tensor_copy(tot[:, :, :], MI[m][:, 256:512].rearrange("p (k c) -> p k c", c=E)), [t])
            for c in range(E):
                a2 = seq(lambda e, c=c: e.tensor_tensor_scan(incl[:, :, c], tot[:, :, c], kc(K_Z, NK), 0.0, ALU.add,
                                                             ALU.add), [a])
            a = seq(lambda e: e.tensor_tensor(
                cmpn[:, :, :], incl[:, NK - 1, :].unsqueeze(2).to_broadcast([P, E, 32]),
                kc(K_J, 32).unsqueeze(1).to_broadcast([P, E, 32]), ALU.is_gt), [a2])
            a = seq(lambda e: e.tensor_reduce(ntl[:, :], cmpn[:, :, :], AX, ALU.add), [a])
            a = seq(lambda e: e.tensor_tensor_scan(tend[:, :], ntl[:, :], kc(K_Z, E), 0.0, ALU.add, ALU.add), [a])
            a3 = seq(lambda e: e.tensor_tensor(tst[:, :], tend[:, :], ntl[:, :], ALU.subtract), [a])
            a = seq(lambda e: e.tensor_tensor(incl[:, :, :], incl[:, :, :], tot[:, :, :], ALU.subtract), [a2])
            a = seq(lambda e: e.scalar_tensor_tensor(
                out=incl[:, :, :], in0=tst[:, :].unsqueeze(1).to_broadcast([P, NK, E]), scalar=float(P),
                in1=incl[:, :, :], op0=ALU.mult, op1=ALU.add), [a, a3])
            a = seq(lambda e: e.tensor_tensor(incl[:, :, :], MI[m][:, 0:256].rearrange("p (k c) -> p k c", c=E),
                                              incl[:, :, :], ALU.add), [a])
            mi_free[m] = [a]
            a = seq(lambda e: e.tensor_tensor(incl[:, :, :], incl[:, :, :], oh[:, :, :], ALU.mult), [a])
            a = seq(lambda e: e.tensor_reduce(posf[:, :], incl[:, :, :], AX, ALU.add), [a])
            st["pos"] = seq(lambda e: e.tensor_copy(posi[:, :], posf[:, :]), [a])
            a = seq(lambda e: e.tensor_tensor(
                cmpt[:, :, :], kc(K_T, NT).unsqueeze(2).to_broadcast([P, NT, E]),
                tend[:, :].unsqueeze(1).to_broadcast([P, NT, E]), ALU.is_ge), [a3])
            a = seq(lambda e: e.tensor_reduce(et[:, :], cmpt[:, :, :], AX, ALU.add), [a])
            a = seq(lambda e: e.tensor_scalar(et[:, :], et[:, :], float(E - 1), float(P), ALU.min, ALU.mult), [a])
            a = seq(lambda e: e.tensor_scalar(et[:, :], et[:, :], kc(K_P, 1), None, ALU.add), [a])
            st["widx"] = seq(lambda e: e.tensor_copy(widx[:, :], et[:, :]), [a])

        def weights(t):
            st["wt", t] = dma("gpsimd", lambda e: e.indirect_dma_start(
                out=wt[t % 2][:, :], out_offset=None, in_=tab_d,
                in_offset=bass.IndirectOffsetOnAxis(ap=widx[:, t:t + 1], axis=0)),
                [st["widx"], st.get(("y", t - 2)), st.get(("hh", t - 2))], f"ld_wt{t % 2}")

        def scatter():
            for k in range(NK):
                st["scat"] = dma("gpsimd", lambda e, k=k: e.indirect_dma_start(
                    out=xs_d, out_offset=bass.IndirectOffsetOnAxis(ap=posi[:, k:k + 1], axis=0),
                    in_=xh[:, k, :], in_offset=None),
                    [st["pos"], zero_x] + [st["h", b] for b in range(NB)], "scat")

        def load_tile(t):
            st["xt", t] = dma("sync", lambda e: e.dma_start(xt[t % 2][:, :], xs_d[t * P:t * P + P, :]),
                              [st["scat"], st.get(("xT", t - 2))], f"ld_xt{t % 2}")

        def ffn_in(t):
            m = misc()
            p = do("tensor", lambda e: e.transpose(MI[m][:, 0:P], xt[t % 2][:, :], idf), [st["xt", t]] + mi_free[m],
                   "p_xT")
            st["xT", t] = p
            w = wt[t % 2]
            st["hT", t] = do("vector", lambda e: e.tensor_scalar(
                hT[:, t % 2, :], MI[m][:, 0:P], w[:, C_G:C_G + 1], w[:, C_B:C_B + 1], ALU.mult, ALU.add),
                [p, st["wt", t], st.get(("h", t - 2, "mm"))], "v_hT")
            mi_free[m] = [st["hT", t]]

        def ffn_up(t):
            m, w = misc(), wt[t % 2]
            for c in range(4):
                p = do("tensor", lambda e, c=c: e.matmul(
                    MI[m][:, c * P:c * P + P], w[:, C_W1 + c * P:C_W1 + c * P + P], hT[:, t % 2, :],
                    start=True, stop=True), [st["hT", t], st["wt", t]] + mi_free[m], "p_h")
            st["h", t, "mm"] = p
            for c in range(4):
                a = do("scalar", lambda e, c=c: e.activation(
                    h1[:, t % 2, c, :], MI[m][:, c * P:c * P + P], ACT.Relu, bias=w[:, C_B1 + c:C_B1 + c + 1]),
                    [p, st.get(("y", t - 2))], "a_h")
            mi_free[m] = [a]
            st["hh", t] = a

        def ffn_down(t):
            m, w = misc(), wt[t % 2]
            for c in range(4):
                do("tensor", lambda e, c=c: e.matmul(
                    MI[m][:, 0:D], h1[:, t % 2, c, :], w[:, C_W2 + c * P:C_W2 + c * P + P], start=(c == 0),
                    stop=False), [st["hh", t]] + mi_free[m])
            p = do("tensor", lambda e: e.matmul(MI[m][:, 0:D], cst[0:1, K_ONE:K_ONE + P], w[0:1, C_B2:C_B2 + D],
                                                start=False, stop=True), sem="p_y")
            st["y", t] = p
            a = do("scalar", lambda e: e.activation(yt[:, t % 2, :], MI[m][:, 0:D], ACT.Copy),
                   [p, st.get(("yst", t - 2))], "a_y")
            mi_free[m] = [a]
            st["yst", t] = dma("sync", lambda e: e.dma_start(ys_d[t * P:t * P + P, :], yt[:, t % 2, :]), [a],
                               f"st_y{t % 2}")

        mxn, scn = [0], [0]
        mx_free, sc_free = [None, None], [None, None]

        def max_units(n):
            b, g = n // NG, n % NG
            u, q = b % 2, n % 2
            def unit(i, hs):
                def emit():
                    k = mxn[0] % 2
                    mxn[0] += 1
                    w = (i + 1) * P
                    for j, h in enumerate(hs):
                        do("tensor", lambda e, j=j, h=h: e.matmul(
                            MX[k][:, j * w:j * w + w], Qop[0:MROW, u, 4 * g + h, i * P:i * P + P],
                            Kop[0:MROW, u, g, 0:w], start=True, stop=False), [st["op", b], mx_free[k]])
                        t = do("tensor", lambda e, j=j: e.matmul(
                            MX[k][:, j * w + i * P:j * w + w], idb[:, :], maskb[:, :], start=False, stop=True),
                            [consts], sem="p_mx")
                    mx_free[k] = do("vector", lambda e: e.tensor_reduce(
                        mx[:, q, i, hs[0]:hs[0] + len(hs)],
                        MX[k][:, 0:w * len(hs)].rearrange("p (h t) -> p h t", t=w), AX, ALU.max),
                        [t, st.get(("nm", n - 2))], "v_mx")
                    st["mx", n] = mx_free[k]
                return emit
            return ([unit(3, [h]) for h in range(4)] + [unit(2, [h]) for h in range(4)]
                    + [unit(1, [0, 1]), unit(1, [2, 3]), unit(0, [0, 1, 2, 3])])

        def max_split(n):
            q = n % 2
            a = do("vector", lambda e: e.tensor_scalar(nm[:, q, :, 0, :], mx[:, q, :, :], -1.0, None, ALU.mult),
                   [st["mx", n], st.get(("mTp", n - 2))], "v_nm")
            st["nm", n] = do("vector", lambda e: e.scalar_tensor_tensor(
                out=nm[:, q, :, 1, :], in0=mx[:, q, :, :], scalar=-1.0, in1=nm[:, q, :, 0, :], op0=ALU.mult,
                op1=ALU.subtract), [a], "v_nm")

        def max_rows(n):
            b, g = n // NG, n % NG
            u, q, m = b % 2, n % 2, misc()
            pt = MI[m][:, :].bitcast(BF16)
            for i in range(NI):
                t = do("tensor", lambda e, i=i: e.transpose(
                    pt[0:8, i * P:i * P + P], nm[:, q, i, :, :].rearrange("p a h -> p (a h)"), idb[:, :]),
                    [st["nm", n]] + mi_free[m], "p_mT")
            st["mTp", n] = t
            a = do("scalar", lambda e: e.activation(mT[:, q, :], pt[0:8, 0:S], ACT.Copy), [t, st.get(("m", n - 2))], "a_mT")
            mi_free[m] = [a]
            for r in range(2):
                st["m", n] = dma("sync", lambda e, r=r: e.dma_start(
                    Qop[MROW + r:MROW + r + 1, u, 4 * g:4 * g + 4, :], mT[4 * r:4 * r + 4, q, :]),
                    [a, st.get(("scored", b - 2, g)), z_o], f"ld_m{q}")

        OFF = [0, 2048, 2048 + 1536, 2048 + 1536 + 1024]

        def score_units(n):
            b, g = n // NG, n % NG
            u, q = b % 2, n % 2
            def unit(j, hs, last):
                def emit():
                    k = scn[0] % 2
                    scn[0] += 1
                    w = S - j * P
                    o = OFF[j] + hs[0] * w
                    t = do("tensor", lambda e: e.matmul(
                        SC[k][:, 0:w * len(hs)].rearrange("p (h s) -> p h s", s=w),
                        Kop[:, u, g, j * P:j * P + P], Qop[:, u, 4 * g + hs[0]:4 * g + hs[0] + len(hs), j * P:S],
                        start=True, stop=True), [st["m", n], st["op", b], sc_free[k]], "p_sc2")
                    st["scored", b, g] = t
                    sc_free[k] = do("scalar", lambda e: e.activation(
                        PT[q][:, o:o + w * len(hs)], SC[k][:, 0:w * len(hs)], ACT.Exp, scale=SCALE),
                        [t, st.get(("pv", n - 2))], "a_ex")
                    if last:
                        blk = PT[q][:, OFF[j]:OFF[j] + 4 * w].rearrange("p (h s) -> p h s", s=w)[:, :, 0:P]
                        st["P", n, j] = do("gpsimd", lambda e: e.affine_select(
                            out=blk, in_=blk, compare_op=ALU.is_ge, fill=0.0, base=0,
                            pattern=[[0, 4], [1, P]], channel_multiplier=-1), [sc_free[k]], "g_mask")
                return emit
            return ([unit(0, [h], h == 3) for h in range(4)] + [unit(1, [h], h == 3) for h in range(4)]
                    + [unit(2, [0, 1], False), unit(2, [2, 3], True), unit(3, [0, 1, 2, 3], True)])

        def pv_units(n):
            b, g = n // NG, n % NG
            q = n % 2
            def unit(j):
                def emit():
                    w = S - j * P
                    for h in range(4):
                        t = do("tensor", lambda e, h=h: e.matmul(
                            PV[32 * h:32 * h + 32, j * P:S], V[:, NI * b + j, g, :],
                            PT[q][:, OFF[j] + h * w:OFF[j] + h * w + w], start=(j == 0), stop=(j == 3),
                            skip_group_check=True),
                            [st["P", n, j], st["V", b], st.get(("O", n - 1))], "p_pv")
                    st["pv", n] = t
                    if j == 3:
                        st["O", n] = do("scalar", lambda e: e.activation(O[:, q, :], PV[:, :], ACT.Copy),
                                        [t, st.get(("Ot", n - 2))], "a_O")
                return emit
            return [unit(j) for j in range(4)]

        def heads(n):
            b, g = n // NG, n % NG
            q, m = n % 2, misc()
            for i in range(NI):
                t = do("tensor", lambda e, i=i: e.transpose(MI[m][:, i * P:i * P + P], O[:, q, i * P:i * P + P], idf),
                       [st["O", n]] + mi_free[m], "p_Ot")
            st["Ot", n] = t
            v = MI[m][:, :].rearrange("p (i h c) -> p i h c", i=NI, h=4)
            r = do("vector", lambda e: e.reciprocal(rden[:, q, :, :], v[:, :, :, 8]), [t], "v_rd")
            st["att", b] = do("vector", lambda e: e.tensor_tensor(
                att[:, b % 2, :, 32 * g:32 * g + 32].rearrange("p i (h d) -> p i h d", h=4), v[:, :, :, 0:8],
                rden[:, q, :, :].unsqueeze(3).to_broadcast([P, NI, 4, 8]), ALU.mult),
                [r, st.get(("aT", b - 2))], "v_att")
            mi_free[m] = [st["att", b]]

        def mix(b):
            u, k0 = b % 2, NI * b
            m, m2 = misc(), misc()
            for i in range(NI):
                t = do("tensor", lambda e, i=i: e.transpose(MI[m][:, i * P:i * P + P], att[:, u, i, :], idf),
                       [st["att", b]] + mi_free[m], "p_aT")
            st["aT", b] = t
            c = do("scalar", lambda e: e.activation(attT[:, :], MI[m][:, :], ACT.Copy), [t, st.get("wo")], "a_aT")
            mi_free[m] = [c]
            for i in range(NI):
                t = do("tensor", lambda e, i=i: e.matmul(MI[m2][:, i * P:i * P + P], attT[:, i * P:i * P + P],
                                                         wo[:, :], start=True, stop=True),
                       [c, l_w] + mi_free[m2], "p_wo")
            st["wo"] = t
            xv = X[:, k0:k0 + NI, :].rearrange("p i d -> p (i d)")
            st["acc", b] = do("vector", lambda e: e.tensor_tensor(xv, MI[m2][:, :], xv, ALU.add),
                              [t, st["xs", b]], "v_acc")
            mi_free[m2] = [st["acc", b]]

        def gather(b):
            for i in range(NI):
                st["yg", b] = dma("gpsimd", lambda e, i=i: e.indirect_dma_start(
                    out=xh[:, NI * b + i, :], out_offset=None, in_=ys_d,
                    in_offset=bass.IndirectOffsetOnAxis(ap=posi[:, NI * b + i:NI * b + i + 1], axis=0)),
                    [st["yst", NT - 1], st["yst", NT - 2], st["scat"]], f"ld_yg{b}")

        def finish(b):
            for i in range(NI):
                k = NI * b + i
                a = do("vector", lambda e, k=k, i=i: e.scalar_tensor_tensor(
                    out=X[:, k, :], in0=xh[:, k, :], scalar=alpha[:, k:k + 1], in1=X[:, k, :], op0=ALU.mult,
                    op1=ALU.add), [st["yg", b], st["alpha"], st["acc", b]], "v_fin")
            st["fin", b] = a
            st["out"] = dma("sync", lambda e: e.dma_start(
                out_d[b].rearrange("(i p) d -> p i d", p=P), X[:, NI * b:NI * b + NI, :]), [a], "st_out")

        NS = NB * NG
        for b in range(NB):
            norm(b)
            rope(b, "vector" if b < 2 else "gpsimd")
            project(b)
            if b < 2:
                operands(b)
            if b == 0:
                pass
        route()
        scatter()
        tiles = list(range(NT))
        weights(0)
        weights(1)
        load_tile(0)
        load_tile(1)
        todo = []
        for t in tiles:
            todo += [lambda t=t: ffn_in(t), lambda t=t: ffn_up(t)]
            def last(t=t):
                ffn_down(t)
                if t + 2 < NT:
                    weights(t + 2)
                    load_tile(t + 2)
            todo.append(last)
        FIRST = 4
        gath = 0
        fin = 0
        for r in range(NS + 5):
            mxu = max_units(r) if r < NS else []
            scu = score_units(r - 2) if 0 <= r - 2 < NS else []
            pvu = pv_units(r - 3) if 0 <= r - 3 < NS else []
            if r % NG == 2 and 2 <= r // NG + 1 < NB:
                operands(r // NG + 1)
            for s in range(11):
                if s == 1 and 0 <= r - 1 < NS:
                    max_rows(r - 1)
                if s < len(scu):
                    scu[s]()
                if s < len(mxu):
                    mxu[s]()
                if s % 3 == 0 and pvu:
                    pvu[s // 3]()
                if s == 2 and 0 <= r - 4 < NS:
                    heads(r - 4)
                if s == 5 and 0 <= r - 4 < NS and (r - 4) % NG == NG - 1:
                    mix((r - 4) // NG)
                if r >= FIRST and s % 2 == 1 and todo:
                    todo.pop(0)()
            if r < NS:
                max_split(r)
            if not todo:
                while gath < NB and gath < fin + 2:
                    gather(gath)
                    gath += 1
                if fin < gath and ("acc", fin) in st and gath > fin + 1:
                    finish(fin)
                    fin += 1
        while todo:
            todo.pop(0)()
        while fin < NB:
            while gath < NB and gath < fin + 2:
                gather(gath)
                gath += 1
            finish(fin)
            fin += 1
        fl.wait("sync", [st["out"], st["yst", NT - 1], st["yst", NT - 2], st["scat"], zero_x,
                         st["q", 0], st["q", 1], st["k", 0], st["k", 1]])
        fl.run(ctx.enter_context(nc.Block()))


def kernel(**inputs):
    import concourse.bacc as bacc
    from concourse.bass_utils import run_bass_kernel_spmd

    a = {k[3:]: np.asarray(v) for k, v in inputs.items()}
    f32 = np.float32
    tab = np.zeros((E, P, ROW), f32)
    tab[:, :, C_W1:C_W1 + F] = a["ffn_W1"].transpose(0, 2, 1)
    tab[:, :, C_W2:C_W2 + F] = a["ffn_W2"].transpose(0, 2, 1).reshape(E, 4, P, D).transpose(0, 2, 1, 3).reshape(E, P, F)
    tab[:, :, C_G] = a["ffn_gamma"]
    tab[:, :, C_B] = a["ffn_beta"]
    tab[:, :, C_B1:C_B1 + 4] = a["ffn_b1"].reshape(E, 4, P).transpose(0, 2, 1)
    tab[:, :, C_B2:C_B2 + D] = a["ffn_b2"][:, None, :]
    cst = np.zeros((P, KW), f32)
    p = np.arange(P)
    cst[:, K_ID:K_ID + P] = np.eye(P)
    cst[:, K_MASK:K_MASK + P] = np.where(p[None, :] > p[:, None], -1e30, 0.0)
    cst[:, K_TRI:K_TRI + P] = p[:, None] < p[None, :]
    cst[:, K_ONE:K_ONE + P] = 1.0
    theta = (f32(1.0) / f32(10000.0) ** (np.arange(64, dtype=f32) / f32(64))).astype(f32)
    ang = np.arange(S, dtype=f32)[:, None] * theta[None, :]
    for k, fn in ((K_COS, np.cos), (K_SIN, np.sin)):
        cst[:, k:k + 256] = fn(ang).astype(f32).reshape(NI, P, 64).transpose(1, 0, 2).reshape(P, 256)
    cst[:, K_IE:K_IE + E] = np.arange(E)
    cst[:, K_IE8:K_IE8 + E] = np.arange(E) + 8
    cst[:, K_J:K_J + 32] = np.arange(32) * P
    cst[:, K_T:K_T + NT] = np.arange(NT)
    cst[:, K_P] = p
    arrays = {
        "X": a["attn_X"],
        "wq": a["attn_W_q"].T,
        "wkv": np.concatenate([a["attn_W_k"], a["attn_W_v"]]).T,
        "wo": a["attn_W_o"].T,
        "cen": a["ffn_centroids"].T,
        "tab": tab.reshape(E * P, ROW),
        "cst": cst,
    }
    arrays = {"in_" + k: np.ascontiguousarray(v) for k, v in arrays.items()}
    nc = bacc.Bacc("TRN2", target_bir_lowering=False, num_devices=1)
    args = [nc.dram_tensor(k, v.shape, mybir.dt.from_np(v.dtype), kind="ExternalInput").ap() for k, v in arrays.items()]
    out = nc.dram_tensor("out", (NB, S, D), F32, kind="ExternalOutput").ap()
    build(nc, *args, out)
    r = run_bass_kernel_spmd(nc, [arrays], core_ids=[0])
    return r.results[0]["out"]
```

```python
from contextlib import ExitStack

import numpy as np

import concourse.bass as bass
from concourse import mybir

F32 = mybir.dt.float32
BF16 = mybir.dt.bfloat16
I32 = mybir.dt.int32
ALU = mybir.AluOpType
ACT = mybir.ActivationFunctionType
AX = mybir.AxisListType.X

P = 128
NB = 8
NI = 4
NK = NB * NI
S = 512
D = 128
NH = 16
NG = 4
E = 8
F = 512
EPS = 1e-5
SCALE = 1.0 / float(np.sqrt(np.float32(8)))
NT = (NK * P + E * (P - 1)) // P
ROW = 1168
C_W1, C_W2, C_G, C_B, C_B1, C_B2 = 0, 512, 1024, 1025, 1026, 1040
K_ID, K_TRI, K_ONE, K_COS, K_SIN, K_MASK = 0, 128, 256, 512, 768, 1177
K_IE, K_IE8, K_J, K_T, K_P, K_Z, K_TOK = 1024, 1032, 1040, 1072, 1112, 1113, 1145
KW = 1177 + 512
XW = D + 2
NY = NK * P + NT * P
SPLIT = [(a, c) for a in range(3) for c in range(3)]
MROW = 96


class Flow:

    ENGINES = ("sync", "gpsimd", "scalar", "tensor", "vector")

    def __init__(self, nc, ctx):
        self.nc, self.ctx = nc, ctx
        self.queue = {e: [] for e in self.ENGINES}
        self.count, self.sems = {}, {}
        self.waited = {e: {} for e in self.ENGINES}

    def mark(self, sem, step):
        if sem not in self.sems:
            self.sems[sem] = self.ctx.enter_context(self.nc.semaphore(sem))
            self.count[sem] = 0
        self.count[sem] += step
        return sem, self.count[sem]

    def wait(self, eng, after):
        for m in after:
            if m is not None and self.waited[eng].get(m[0], 0) < m[1]:
                self.waited[eng][m[0]] = m[1]
                self.queue[eng].append(lambda e, s=self.sems[m[0]], v=m[1]: e.wait_ge(s, v))

    def do(self, eng, fn, after=(), sem=None, step=1):
        self.wait(eng, after)
        if sem is None:
            self.queue[eng].append(fn)
            return None
        m = self.mark(sem, step)
        self.queue[eng].append(lambda e, s=self.sems[sem]: fn(e).then_inc(s, step))
        return m

    def dma(self, eng, fn, after=(), sem=None):
        return self.do(eng, fn, after, sem, 16)

    def run(self, block):
        for name in self.ENGINES:
            def body(e, q=self.queue[name]):
                for f in q:
                    f(e)
            (block.sync if name == "sync" else block.gpsimd if name == "gpsimd" else block.scalar if name == "scalar"
             else block.tensor if name == "tensor" else block.vector)(body)


def build(nc, X_d, wq_d, wkv_d, wo_d, cen_d, tab_d, cst_d, out_d):
    with ExitStack() as ctx:
        fl = Flow(nc, ctx)
        do, dma = fl.do, fl.dma

        def sb(name, shape, dt=F32):
            return ctx.enter_context(nc.sbuf_tensor(name, shape, dt))

        def ps(name, shape, dt=F32):
            return ctx.enter_context(nc.psum_tensor(name, shape, dt))

        def dram(name, shape, dt=F32):
            return nc.dram_tensor(name, shape, dt, kind="Internal").ap()

        xs_d = dram("xs_d", (NT * P, XW))
        ys_d = dram("ys_d", (NY, D))
        qd = [dram(f"qd{b}", (P, 3, S), BF16) for b in range(NB)]
        kd = [dram(f"kd{b}", (32, 3, S), BF16) for b in range(NB)]

        cst = sb("cst", [P, KW])
        idf = cst[:, K_ID:K_ID + P]
        idb = sb("idb", [P, P], BF16)
        trib = sb("trib", [P, P], BF16)
        oneb = sb("oneb", [P, P], BF16)
        cosT = cst[:, K_COS:K_COS + 256].rearrange("p (i c) -> p i c", i=NI)
        sinT = cst[:, K_SIN:K_SIN + 256].rearrange("p (i c) -> p i c", i=NI)
        wq = sb("wq", [P, P])
        wkv = sb("wkv", [P, 64])
        wo = sb("wo", [P, P])
        cen = sb("cen", [P, E])
        X = sb("X", [P, NK, D])
        xh = sb("xh", [P, NK, XW])
        xr = sb("xr", [P, NK, D])
        rt = sb("rt", [P, NI, 64])
        xnT = sb("xnT", [P, S])
        xrT = sb("xrT", [P, S])
        qp = sb("qp", [P, 1, 3, S], BF16)
        kp = sb("kp", [32, 1, 3, S], BF16)
        qr = sb("qr", [P, S])
        kr = sb("kr", [32, S])
        Qop = sb("Qop", [P, 2, NH, S], BF16)
        Kop = sb("Kop", [P, 2, NG, S], BF16)
        V = sb("V", [P, NK, NG, 32])
        PT = [sb(f"PT{i}", [P, 4 * 1280]) for i in range(2)]
        st1, st2 = sb("st1", [P, NK, 6]), sb("st2", [P, NK, 6])
        mv1, mv2 = sb("mv1", [P, NK, 2]), sb("mv2", [P, NK, 2])
        rs1, rs2 = sb("rs1", [P, NK]), sb("rs2", [P, NK])
        mx = sb("mx", [P, 2, NI, 4])
        nm = sb("nm", [P, 2, NI, 2, 4], BF16)
        mT = sb("mT", [8, 2, S], BF16)
        O = sb("O", [P, 2, S])
        rden = sb("rden", [P, 2, NI, 4])
        att = sb("att", [P, 2, NI, D])
        attT = sb("attT", [P, S])
        xrf = xr[:, :, :].rearrange("p k d -> p (k d)")
        wt = [sb(f"wt{i}", [P, ROW])[:, :] for i in range(2)] + [xrf[:, 0:ROW]]
        xt = [sb(f"xt{i}", [P, XW])[:, :] for i in range(2)] + [xrf[:, ROW:ROW + XW]]
        tid = sb("tid", [P, 3], I32)
        hT = sb("hT", [P, 2, P])
        h1 = sb("h1", [P, 2, 4, P])
        yt = sb("yt", [P, 2, D])
        sc = sb("sc", [P, NK, E])
        smx, sam, alpha, ea = (sb(n, [P, NK]) for n in ("smx", "sam", "alpha", "ea"))
        eq, oh, tot, incl = (sb(n, [P, NK, E]) for n in ("eq", "oh", "tot", "incl"))
        ohb = sb("ohb", [P, NK, E], BF16)
        cmpn = sb("cmpn", [P, E, 32])
        ntl, tend, tst = (sb(n, [P, E]) for n in ("ntl", "tend", "tst"))
        cmpt = sb("cmpt", [P, NT, E])
        et = sb("et", [P, NT])
        posf = sb("posf", [P, NK])
        posi = sb("posi", [P, NK], I32)
        widx = sb("widx", [P, NT], I32)

        MX = [ps(f"MX{i}", [P, 512]) for i in range(2)]
        SC = [ps(f"SC{i}", [P, 512]) for i in range(2)]
        PV = ps("PV", [P, 512])
        MI = [ps(f"MI{i}", [P, 512]) for i in range(3)]

        banks = {"next": 0, "free": [[], [], []], "held": [False] * 3}
        pending = []
        clock = [0]

        def later(slots, fn):
            if clock[0] == 0:
                fn()
            else:
                pending.append((clock[0] + slots, len(pending), fn))

        def tick():
            clock[0] += 1
            while any(p[0] <= clock[0] for p in pending):
                first_pending()

        def first_pending():
            p = min(pending, key=lambda x: x[0])
            pending.remove(p)
            p[2]()

        def misc():
            k = banks["next"] % 3
            banks["next"] += 1
            while banks["held"][k]:
                first_pending()
            banks["held"][k] = True
            return k

        def release(k, mark):
            banks["held"][k] = False
            banks["free"][k] = [mark]

        mi_free = banks["free"]

        x_in = []
        for b in range(NB):
            x_in.append(dma("sync", lambda e, b=b: e.dma_start(
                X[:, NI * b:NI * b + NI, :], X_d[b].rearrange("(i p) d -> p i d", p=P)), sem=f"l_x{b}"))
            if b == 0:
                l_c = dma("sync", lambda e: e.dma_start(cst[:, :], cst_d), sem="l_cst")
                for t, s in ((cen, cen_d), (wq, wq_d), (wkv, wkv_d), (wo, wo_d)):
                    l_w = dma("sync", lambda e, t=t, s=s: e.dma_start(t[:, :], s), sem="l_w")
        consts = None
        for t, k in ((idb, K_ID), (trib, K_TRI), (oneb, K_ONE)):
            consts = do("scalar", lambda e, t=t, k=k: e.activation(t[:, :], cst[:, k:k + P], ACT.Copy),
                        [l_c], "consts")
        z_v0 = do("gpsimd", lambda e: e.memset(V[:, 0:NI, :, :], 1.0), sem="clr")
        z_k, z_q = [], []
        for u in range(2):
            z = do("gpsimd", lambda e, u=u: e.memset(Kop[:, u, :, :].bitcast(F32), 0.0), sem="clr")
            z_k.append(do("gpsimd", lambda e, u=u: e.memset(Kop[MROW:MROW + 2, u, :, :], 1.0), [z], "clr"))
            z_q.append(do("gpsimd", lambda e, u=u: e.memset(Qop[:, u, :, :].bitcast(F32), 0.0), [z_k[u]], "clr"))
        z_v = do("gpsimd", lambda e: e.memset(V[:, NI:NK, :, :], 1.0), sem="clr")
        blank = PT[1][:, 0:NT * XW].rearrange("p (t d) -> p t d", t=NT)
        z = do("gpsimd", lambda e: e.memset(blank, 0.0), sem="clr")
        z = do("gpsimd", lambda e: e.tensor_scalar(
            blank[:, :, D], cst[:, K_T:K_T + NT], float(P), cst[:, K_P:K_P + 1], ALU.mult, ALU.add), [z, l_c], "clr")
        z = do("gpsimd", lambda e: e.tensor_scalar(blank[:, :, D], blank[:, :, D], float(NK * P), None, ALU.add),
               [z], "clr")
        zero_x = dma("sync", lambda e: e.dma_start(xs_d.rearrange("(t p) d -> p t d", p=P), blank), [z], "zx")
        do("gpsimd", lambda e: e.memset(xh[:, :, D + 1], 0.0), sem="clr")
        z_tok = do("gpsimd", lambda e: e.tensor_copy(xh[:, :, D], cst[:, K_TOK:K_TOK + NK]), sem="clr")

        st = {}

        def stats(which, b0, b1):
            dst, mv = (st1, mv1) if which == 1 else (st2, mv2)
            ks = range(NI * b0, NI * b1)
            for k in ks:
                src = X[:, k, :] if which == 1 else xh[:, k, 0:D]
                a = do("vector", lambda e, k=k, src=src: e.bn_stats(dst[:, k, :], src),
                       [x_in[k // NI] if which == 1 else st["n", k // NI]], "v_ln")
            for k in ks:
                a2 = do("vector", lambda e, k=k: e.bn_aggr(mv[:, k, :], dst[:, k, :]), [a], "v_ln")
            if which == 1:
                invert(1, b0, b1, a2)
            st["mv", which] = a2

        def invert(which, b0, b1, after):
            mv, rs = (mv1, rs1) if which == 1 else (mv2, rs2)
            r = rs[:, NI * b0:NI * b1]
            a = do("vector", lambda e: e.tensor_scalar(r, mv[:, NI * b0:NI * b1, 1], EPS, None, ALU.add), [after],
                   "v_ln")
            a = do("scalar", lambda e: e.activation(r, r, ACT.Sqrt), [a], "a_ln")
            a = do("vector", lambda e: e.reciprocal(r, r), [a], "v_ln")
            for b in range(b0, b1):
                st["rs", which, b] = a

        def stats2(b):
            stats(2, b, b + 1)

        def rstd2():
            invert(2, 0, NB, st["mv", 2])

        def norm(b):
            for k in range(NI * b, NI * b + NI):
                st["n", b] = do("vector", lambda e, k=k: e.tensor_scalar(
                    xh[:, k, 0:D], X[:, k, :], mv1[:, k, 0:1], rs1[:, k:k + 1], ALU.subtract, ALU.mult),
                    [st["rs", 1, b]], "v_ln")

        def residual(b):
            k0 = NI * b
            st["xs", b] = do("gpsimd", lambda e: e.tensor_tensor(
                X[:, k0:k0 + NI, :], X[:, k0:k0 + NI, :], xh[:, k0:k0 + NI, 0:D], ALU.add), [st["n", b]], "g_xs")

        def renorm(b):
            for k in range(NI * b, NI * b + NI):
                st["h", b] = do("vector", lambda e, k=k: e.tensor_scalar(
                    xh[:, k, 0:D], xh[:, k, 0:D], mv2[:, k, 0:1], rs2[:, k:k + 1], ALU.subtract, ALU.mult),
                    [st["rs", 2, b], st["r", b], st["xs", b], st["xnTp", b]], "v_xh")

        def router_in(b):
            k0, m = NI * b, misc()
            for i in range(NI):
                t = do("tensor", lambda e, i=i: e.transpose(MI[m][:, i * P:i * P + P], xh[:, k0 + i, 0:D], idf),
                       [l_c, st["n", b]] + mi_free[m], "p_xnT")
            st["xnTp", b] = t

            def read():
                st["xnTc"] = do("scalar", lambda e: e.activation(xnT[:, :], MI[m][:, :], ACT.Copy),
                                [t, st.get("xnT")], "a_xnT")
                release(m, st["xnTc"])
            later(1, read)

        def router(b):
            k0, m = NI * b, misc()
            for i in range(NI):
                t = do("tensor", lambda e, i=i: e.matmul(MI[m][:, i * E:i * E + E], xnT[:, i * P:i * P + P],
                                                         cen[:, :], start=True, stop=True),
                       [st["xnTc"], l_w] + mi_free[m], "p_sc")
            st["xnT"] = t

            def read():
                st["sc"] = do("vector", lambda e: e.tensor_copy(
                    sc[:, k0:k0 + NI, :], MI[m][:, 0:NI * E].rearrange("p (i c) -> p i c", i=NI)), [t], "v_sc")
                release(m, st["sc"])
            later(1, read)

        def rope(b, eng):
            v = xh[:, NI * b:NI * b + NI, 0:D].rearrange("p i (c two) -> p i c two", two=2)
            xe, xo = v[:, :, :, 0], v[:, :, :, 1]
            lo, hi = xr[:, NI * b:NI * b + NI, 0:64], xr[:, NI * b:NI * b + NI, 64:128]
            sem = "v_rope" if eng == "vector" else "g_rope"
            w = [st["n", b], l_c, st.get("rt")]
            do(eng, lambda e: e.tensor_tensor(lo, xe, cosT, ALU.mult), w, sem)
            a = do(eng, lambda e: e.tensor_tensor(rt[:, :, :], xo, sinT, ALU.mult), w, sem)
            a = do(eng, lambda e: e.tensor_tensor(lo, lo, rt[:, :, :], ALU.subtract), [a], sem)
            do(eng, lambda e: e.tensor_tensor(hi, xe, sinT, ALU.mult), sem=sem)
            a = do(eng, lambda e: e.tensor_tensor(rt[:, :, :], xo, cosT, ALU.mult), [a], sem)
            a = do(eng, lambda e: e.tensor_tensor(hi, hi, rt[:, :, :], ALU.add), [a], sem)
            st["r", b] = st["rt"] = a

        def project_in(b):
            m = misc()
            for i in range(NI):
                t = do("tensor", lambda e, i=i: e.transpose(MI[m][:, i * P:i * P + P], xr[:, NI * b + i, :], idf),
                       [l_c, st["r", b]] + mi_free[m], "p_xrT")
            st["xrTp", b] = t

            def read():
                st["xrTc"] = do("scalar", lambda e: e.activation(xrT[:, :], MI[m][:, :], ACT.Copy),
                                [t, st.get("xrT")], "a_xrT")
                release(m, st["xrTc"])
            later(1, read)

        def project_v(b):
            k0, m = NI * b, misc()
            for i in range(NI):
                t = do("tensor", lambda e, i=i: e.matmul(MI[m][:, i * 32:i * 32 + 32], xrT[:, i * P:i * P + P],
                                                         wkv[:, 32:64], start=True, stop=True),
                       [st["xrTc"], l_w] + mi_free[m], "p_q")
            st["xrT"] = t

            def read():
                st["V", b] = do("vector", lambda e: e.tensor_copy(
                    V[:, k0:k0 + NI, :, 0:8], MI[m][:, 0:P].rearrange("p (i g d) -> p i g d", i=NI, g=NG)),
                    [t, z_v0 if b == 0 else z_v], "v_v")
                release(m, st["V", b])
            later(1, read)

        def project(b, key):
            u, m = 0, misc()
            w, part, rem, n, dst = (wq[:, :], qp, qr, P, qd[b]) if key == "q" else (wkv[:, 0:32], kp, kr, 32, kd[b])
            src = MI[m]
            t = do("tensor", lambda e: e.matmul(src[0:n, :], w, xrT[:, :], start=True, stop=True),
                   [st["xrTc"], l_w] + mi_free[m], "p_q")
            st["xrT"] = t

            def part0():
                a = do("scalar", lambda e: e.activation(part[0:n, u, 0, :], src[0:n, :], ACT.Copy),
                       [t, st.get((key, u))], "a_sp")
                later(1, lambda: rest1(a))

            def rest1(a):
                v = do("vector", lambda e: e.tensor_tensor(rem[0:n, :], src[0:n, :], part[0:n, u, 0, :], ALU.subtract),
                       [a, st.get((key, "r"))], "v_sp")
                release(m, v)
                later(1, lambda: part1(v))

            def part1(v):
                a = do("scalar", lambda e: e.activation(part[0:n, u, 1, :], rem[0:n, :], ACT.Copy), [v], "a_sp")
                later(1, lambda: part2(a))

            def part2(a):
                v = do("vector", lambda e: e.tensor_tensor(part[0:n, u, 2, :], rem[0:n, :], part[0:n, u, 1, :],
                                                           ALU.subtract), [a], "v_sp")
                st[key, "r"] = v
                st[key, u] = dma("sync", lambda e: e.dma_start(dst, part[0:n, u, :, :]), [v], f"st_{key}{u}")
            later(1, part0)

        def operands(b):
            u = b % 2
            free = [z_k[u], z_q[u]] + [st.get(("scored", b - 2, g)) for g in range(NG)]
            for r, (a, c) in enumerate(SPLIT):
                dma("sync", lambda e, r=r, a=a: e.dma_start(
                    Qop[8 * r:8 * r + 8, u, :, :], qd[b][:, a, :].rearrange("(h d) t -> d h t", d=8)),
                    [st["q", 0]] + free, f"ld_op{u}")
                st["op", b] = dma("sync", lambda e, r=r, c=c: e.dma_start(
                    Kop[8 * r:8 * r + 8, u, :, :], kd[b][:, c, :].rearrange("(g d) t -> d g t", d=8)),
                    [st["k", 0]], f"ld_op{u}")

        def route():
            seq = lambda fn, after=(), eng="vector": do(eng, fn, list(after), "v_rt")
            bc = lambda a: a.unsqueeze(2).to_broadcast([P, NK, E])
            kc = lambda o, n: cst[:, o:o + n]
            a = seq(lambda e: e.tensor_reduce(smx[:, :], sc[:, :, :], AX, ALU.max), [st["sc"], l_c])
            x = do("scalar", lambda e: e.activation(ea[:, :], smx[:, :], ACT.Exp, scale=-1.0), [a], "a_al")
            a = seq(lambda e: e.tensor_tensor(eq[:, :, :], sc[:, :, :], bc(smx[:, :]), ALU.is_equal), [a])
            a = seq(lambda e: e.scalar_tensor_tensor(
                out=eq[:, :, :], in0=eq[:, :, :], scalar=-8.0,
                in1=kc(K_IE8, E).unsqueeze(1).to_broadcast([P, NK, E]), op0=ALU.mult, op1=ALU.add), [a])
            a = seq(lambda e: e.tensor_reduce(sam[:, :], eq[:, :, :], AX, ALU.min), [a])
            a = seq(lambda e: e.tensor_tensor(oh[:, :, :], kc(K_IE, E).unsqueeze(1).to_broadcast([P, NK, E]),
                                              bc(sam[:, :]), ALU.is_equal), [a])
            a = seq(lambda e: e.tensor_copy(ohb[:, :, :], oh[:, :, :]), [a])
            m = misc()
            flat = ohb[:, :, :].rearrange("p k c -> p (k c)")
            do("tensor", lambda e: e.matmul(MI[m][:, 0:256], trib[:, :], flat, start=True, stop=True),
               [a, consts] + mi_free[m], "p_rt")
            t = do("tensor", lambda e: e.matmul(MI[m][:, 256:512], oneb[:, :], flat, start=True, stop=True),
                   sem="p_rt")
            a = seq(lambda e: e.tensor_scalar(ea[:, :], ea[:, :], 1.0, None, ALU.add), [x])
            st["alpha"] = seq(lambda e: e.reciprocal(alpha[:, :], ea[:, :]), [a])
            a = seq(lambda e: e.tensor_copy(tot[:, :, :], MI[m][:, 256:512].rearrange("p (k c) -> p k c", c=E)), [t])
            for c in range(E):
                a2 = seq(lambda e, c=c: e.tensor_tensor_scan(incl[:, :, c], tot[:, :, c], kc(K_Z, NK), 0.0, ALU.add,
                                                             ALU.add), [a])
            a = seq(lambda e: e.tensor_tensor(
                cmpn[:, :, :], incl[:, NK - 1, :].unsqueeze(2).to_broadcast([P, E, 32]),
                kc(K_J, 32).unsqueeze(1).to_broadcast([P, E, 32]), ALU.is_gt), [a2])
            a = seq(lambda e: e.tensor_reduce(ntl[:, :], cmpn[:, :, :], AX, ALU.add), [a])
            a = seq(lambda e: e.tensor_tensor_scan(tend[:, :], ntl[:, :], kc(K_Z, E), 0.0, ALU.add, ALU.add), [a])
            a3 = seq(lambda e: e.tensor_tensor(tst[:, :], tend[:, :], ntl[:, :], ALU.subtract), [a])
            a = seq(lambda e: e.tensor_tensor(incl[:, :, :], incl[:, :, :], tot[:, :, :], ALU.subtract), [a2])
            a = seq(lambda e: e.scalar_tensor_tensor(
                out=incl[:, :, :], in0=tst[:, :].unsqueeze(1).to_broadcast([P, NK, E]), scalar=float(P),
                in1=incl[:, :, :], op0=ALU.mult, op1=ALU.add), [a, a3])
            a = seq(lambda e: e.tensor_tensor(incl[:, :, :], MI[m][:, 0:256].rearrange("p (k c) -> p k c", c=E),
                                              incl[:, :, :], ALU.add), [a])
            release(m, a)
            a = seq(lambda e: e.tensor_tensor(incl[:, :, :], incl[:, :, :], oh[:, :, :], ALU.mult), [a])
            a = seq(lambda e: e.tensor_reduce(posf[:, :], incl[:, :, :], AX, ALU.add), [a])
            st["pos"] = seq(lambda e: e.tensor_copy(posi[:, :], posf[:, :]), [a])
            a = seq(lambda e: e.tensor_tensor(
                cmpt[:, :, :], kc(K_T, NT).unsqueeze(2).to_broadcast([P, NT, E]),
                tend[:, :].unsqueeze(1).to_broadcast([P, NT, E]), ALU.is_ge), [a3])
            a = seq(lambda e: e.tensor_reduce(et[:, :], cmpt[:, :, :], AX, ALU.add), [a])
            a = seq(lambda e: e.tensor_scalar(et[:, :], et[:, :], float(E - 1), float(P), ALU.min, ALU.mult), [a])
            a = seq(lambda e: e.tensor_scalar(et[:, :], et[:, :], kc(K_P, 1), None, ALU.add), [a])
            st["widx"] = seq(lambda e: e.tensor_copy(widx[:, :], et[:, :]), [a])

        def weights(t):
            st["wt", t] = dma("gpsimd", lambda e: e.indirect_dma_start(
                out=wt[t % 3], out_offset=None, in_=tab_d,
                in_offset=bass.IndirectOffsetOnAxis(ap=widx[:, t:t + 1], axis=0)),
                [st["widx"], st.get(("y", t - 3)), st["xrTp", 2]], f"ld_wt{t % 3}")

        def scatter(k):
            st["scat"] = dma("gpsimd", lambda e: e.indirect_dma_start(
                out=xs_d, out_offset=bass.IndirectOffsetOnAxis(ap=posi[:, k:k + 1], axis=0),
                in_=xh[:, k, :], in_offset=None),
                [st["pos"], zero_x, z_tok, st["h", k // NI]], "scat")

        def load_tile(t):
            st["xt", t] = dma("sync", lambda e: e.dma_start(xt[t % 3], xs_d[t * P:t * P + P, :]),
                              [st["scat"], st.get(("xT", t - 3)), st.get(("tid", t - 3)), st["xrTp", 2]], f"ld_xt{t % 3}")

        def ffn_in(t):
            m = misc()
            p = do("tensor", lambda e: e.transpose(MI[m][:, 0:P], xt[t % 3][:, 0:D], idf), [st["xt", t]] + mi_free[m],
                   "p_xT")
            st["xT", t] = p
            w = wt[t % 3]

            def read():
                st["hT", t] = do("vector", lambda e: e.tensor_scalar(
                    hT[:, t % 2, :], MI[m][:, 0:P], w[:, C_G:C_G + 1], w[:, C_B:C_B + 1], ALU.mult, ALU.add),
                    [p, st["wt", t], st.get(("h", t - 2, "mm"))], "v_hT")
                release(m, st["hT", t])
                st["tid", t] = do("vector", lambda e: e.tensor_copy(
                    tid[:, t % 3:t % 3 + 1], xt[t % 3][:, D:D + 1]), [st.get(("yst", t - 3))], "v_tid")
            later(1, read)

        def ffn_up(t):
            m, w = misc(), wt[t % 3]
            for c in range(4):
                p = do("tensor", lambda e, c=c: e.matmul(
                    MI[m][:, c * P:c * P + P], w[:, C_W1 + c * P:C_W1 + c * P + P], hT[:, t % 2, :],
                    start=True, stop=True), [st["hT", t], st["wt", t]] + mi_free[m], "p_h")
            st["h", t, "mm"] = p

            def read():
                for c in range(4):
                    a = do("scalar", lambda e, c=c: e.activation(
                        h1[:, t % 2, c, :], MI[m][:, c * P:c * P + P], ACT.Relu, bias=w[:, C_B1 + c:C_B1 + c + 1]),
                        [p, st.get(("ymm", t - 2))], "a_h")
                release(m, a)
                st["hh", t] = a
            later(1, read)

        def ffn_down(t):
            m, w = misc(), wt[t % 3]
            for c in range(4):
                p = do("tensor", lambda e, c=c: e.matmul(
                    MI[m][:, 0:D], h1[:, t % 2, c, :], w[:, C_W2 + c * P:C_W2 + c * P + P], start=(c == 0),
                    stop=(c == 3)), [st["hh", t]] + mi_free[m], "p_y")
            st["ymm", t] = p

            def read():
                st["y", t] = do("vector", lambda e: e.tensor_tensor(
                    yt[:, t % 2, :], MI[m][:, 0:D], w[:, C_B2:C_B2 + D], ALU.add),
                    [p, st.get(("yst", t - 2))], "v_y")
                release(m, st["y", t])
            later(1, read)

        def ffn_out(t):
            st["yst", t] = dma("gpsimd", lambda e: e.indirect_dma_start(
                out=ys_d, out_offset=bass.IndirectOffsetOnAxis(ap=tid[:, t % 3:t % 3 + 1], axis=0),
                in_=yt[:, t % 2, :], in_offset=None), [st["y", t], st["tid", t]], f"st_y{t % 2}")
            if t + 3 < NT:
                weights(t + 3)
                load_tile(t + 3)

        mxn, scn = [0], [0]
        mx_free, sc_free = [None, None], [None, None]

        def max_units(n):
            b, g = n // NG, n % NG
            u, q = b % 2, n % 2
            def unit(i, hs):
                def emit():
                    k = mxn[0] % 2
                    mxn[0] += 1
                    w = (i + 1) * P
                    for j, h in enumerate(hs):
                        t = do("tensor", lambda e, j=j, h=h: e.matmul(
                            MX[k][:, j * w:j * w + w], Qop[0:MROW, u, 4 * g + h, i * P:i * P + P],
                            Kop[0:MROW, u, g, 0:w], start=True, stop=True), [st["op", b], mx_free[k]], "p_mx")
                    for j, h in enumerate(hs):
                        a = do("vector", lambda e, j=j, h=h: e.tensor_tensor_reduce(
                            MX[k][:, j * w:j * w + w], MX[k][:, j * w:j * w + w], cst[:, K_MASK + S - w:K_MASK + S], 1.0, -3e38,
                            ALU.add, ALU.max, mx[:, q, i, h:h + 1]), [t, st.get(("nm", n - 2))], "v_mx")
                    mx_free[k] = st["mx", n] = a
                return emit
            return ([unit(3, [h]) for h in range(4)] + [unit(2, [h]) for h in range(4)]
                    + [unit(1, [0, 1]), unit(1, [2, 3]), unit(0, [0, 1, 2, 3])])

        def max_split(n):
            q = n % 2
            a = do("vector", lambda e: e.tensor_scalar(nm[:, q, :, 0, :], mx[:, q, :, :], -1.0, None, ALU.mult),
                   [st["mx", n], st.get(("mTp", n - 2))], "v_nm")
            st["nm", n] = do("vector", lambda e: e.scalar_tensor_tensor(
                out=nm[:, q, :, 1, :], in0=mx[:, q, :, :], scalar=-1.0, in1=nm[:, q, :, 0, :], op0=ALU.mult,
                op1=ALU.subtract), [a], "v_nm")

        def max_rows(n):
            b, g = n // NG, n % NG
            u, q, m = b % 2, n % 2, misc()
            pt = MI[m][:, :].bitcast(BF16)
            for i in range(NI):
                t = do("tensor", lambda e, i=i: e.transpose(
                    pt[0:8, i * P:i * P + P], nm[:, q, i, :, :].rearrange("p a h -> p (a h)"), idb[:, :]),
                    [st["nm", n]] + mi_free[m], "p_mT")
            st["mTp", n] = t

            def read():
                a = do("scalar", lambda e: e.activation(mT[:, q, :], pt[0:8, 0:S], ACT.Copy),
                       [t, st.get(("m", n - 2))], "a_mT")
                release(m, a)
                for r in range(2):
                    st["m", n] = dma("sync", lambda e, r=r: e.dma_start(
                        Qop[MROW + r:MROW + r + 1, u, 4 * g:4 * g + 4, :], mT[4 * r:4 * r + 4, q, :]),
                        [a, st.get(("scored", b - 2, g)), z_q[u]], f"ld_m{q}")
            later(1, read)

        OFF = [0, 2048, 2048 + 1536, 2048 + 1536 + 1024]

        def score_units(n):
            b, g = n // NG, n % NG
            u, q = b % 2, n % 2
            def unit(j, hs, last):
                def emit():
                    k = scn[0] % 2
                    scn[0] += 1
                    w = S - j * P
                    o = OFF[j] + hs[0] * w
                    t = do("tensor", lambda e: e.matmul(
                        SC[k][:, 0:w * len(hs)].rearrange("p (h s) -> p h s", s=w),
                        Kop[:, u, g, j * P:j * P + P], Qop[:, u, 4 * g + hs[0]:4 * g + hs[0] + len(hs), j * P:S],
                        start=True, stop=True), [st["m", n], st["op", b], sc_free[k]], "p_sc2")
                    st["scored", b, g] = t
                    sc_free[k] = do("scalar", lambda e: e.activation(
                        PT[q][:, o:o + w * len(hs)], SC[k][:, 0:w * len(hs)], ACT.Exp, scale=SCALE),
                        [t, st.get(("pv", n - 2))], "a_ex")
                    if last:
                        blk = PT[q][:, OFF[j]:OFF[j] + 4 * w].rearrange("p (h s) -> p h s", s=w)[:, :, 0:P]
                        st["P", n, j] = do("gpsimd", lambda e: e.affine_select(
                            out=blk, in_=blk, compare_op=ALU.is_ge, fill=0.0, base=0,
                            pattern=[[0, 4], [1, P]], channel_multiplier=-1), [sc_free[k]], "g_mask")
                return emit
            return ([unit(0, [h], h == 3) for h in range(4)] + [unit(1, [h], h == 3) for h in range(4)]
                    + [unit(2, [0, 1], False), unit(2, [2, 3], True), unit(3, [0, 1, 2, 3], True)])

        def pv_units(n):
            b, g = n // NG, n % NG
            q = n % 2
            def unit(j):
                def emit():
                    w = S - j * P
                    for h in range(4):
                        t = do("tensor", lambda e, h=h: e.matmul(
                            PV[32 * h:32 * h + 32, j * P:S], V[:, NI * b + j, g, :],
                            PT[q][:, OFF[j] + h * w:OFF[j] + h * w + w], start=(j == 0), stop=(j == 3),
                            skip_group_check=True),
                            [st["P", n, j], st["V", b], st.get(("O", n - 1))], "p_pv")
                    st["pv", n] = t
                    if j == 3:
                        def read():
                            st["O", n] = do("scalar", lambda e: e.activation(O[:, q, :], PV[:, :], ACT.Copy),
                                            [t, st.get(("Ot", n - 2))], "a_O")
                        later(1, read)
                return emit
            return [unit(j) for j in range(4)]

        def heads(n):
            b, g = n // NG, n % NG
            q, m = n % 2, misc()
            for i in range(NI):
                t = do("tensor", lambda e, i=i: e.transpose(MI[m][:, i * P:i * P + P], O[:, q, i * P:i * P + P], idf),
                       [st["O", n]] + mi_free[m], "p_Ot")
            st["Ot", n] = t
            v = MI[m][:, :].rearrange("p (i h c) -> p i h c", i=NI, h=4)

            def read():
                r = do("vector", lambda e: e.reciprocal(rden[:, q, :, :], v[:, :, :, 8]), [t], "v_rd")
                st["att", b] = do("vector", lambda e: e.tensor_tensor(
                    att[:, b % 2, :, 32 * g:32 * g + 32].rearrange("p i (h d) -> p i h d", h=4), v[:, :, :, 0:8],
                    rden[:, q, :, :].unsqueeze(3).to_broadcast([P, NI, 4, 8]), ALU.mult),
                    [r, st.get(("aT", b - 2))], "v_att")
                release(m, st["att", b])
            later(1, read)

        def mix(b):
            u, m = b % 2, misc()
            for i in range(NI):
                t = do("tensor", lambda e, i=i: e.transpose(MI[m][:, i * P:i * P + P], att[:, u, i, :], idf),
                       [st["att", b]] + mi_free[m], "p_aT")
            st["aT", b] = t

            def read():
                c = do("scalar", lambda e: e.activation(attT[:, :], MI[m][:, :], ACT.Copy), [t, st.get("wo")], "a_aT")
                release(m, c)
                later(1, lambda: product(c))

            def product(c):
                m2 = misc()
                for i in range(NI):
                    t2 = do("tensor", lambda e, i=i: e.matmul(MI[m2][:, i * P:i * P + P], attT[:, i * P:i * P + P],
                                                              wo[:, :], start=True, stop=True),
                            [c, l_w] + mi_free[m2], "p_wo")
                st["wo"] = t2
                later(1, lambda: add(m2, t2))

            def add(m2, t2):
                xv = X[:, NI * b:NI * b + NI, :].rearrange("p i d -> p (i d)")
                st["acc", b] = do("vector", lambda e: e.tensor_tensor(xv, MI[m2][:, :], xv, ALU.add),
                                  [t2, st["xs", b]], "v_acc")
                release(m2, st["acc", b])
            later(1, read)

        def load_y(b):
            st["yg", b] = dma("sync", lambda e: e.dma_start(
                xh[:, NI * b:NI * b + NI, 0:D], ys_d[b * S:b * S + S, :].rearrange("(i p) d -> p i d", p=P)),
                [st["yst", NT - 1], st["yst", NT - 2], st["scat"]], f"ld_yg{b}")

        def finish(b):
            for i in range(NI):
                k = NI * b + i
                a = do("vector", lambda e, k=k, i=i: e.scalar_tensor_tensor(
                    out=X[:, k, :], in0=xh[:, k, 0:D], scalar=alpha[:, k:k + 1], in1=X[:, k, :], op0=ALU.mult,
                    op1=ALU.add), [st["yg", b], st["alpha"], st["acc", b]], "v_fin")
            st["fin", b] = a
            st["out"] = dma("sync", lambda e: e.dma_start(
                out_d[b].rearrange("(i p) d -> p i d", p=P), X[:, NI * b:NI * b + NI, :]), [a], "st_out")

        NS = NB * NG
        stats(1, 0, 1)
        norm(0)
        rope(0, "vector")
        residual(0)
        project_in(0)
        project(0, "k")
        project(0, "q")
        project_v(0)
        operands(0)
        stats(1, 1, NB)
        for b in range(1, NB):
            norm(b)
            if b < 3:
                rope(b, "gpsimd")
                residual(b)
        router_in(0)
        router(0)
        clock[0] = 1
        todo = []

        def first():
            for t in range(3):
                weights(t)
                load_tile(t)

        for t in range(NT + 1):
            if t < NT:
                todo.append(lambda t=t: ffn_in(t))
            if t > 0:
                todo.append(lambda t=t: ffn_down(t - 1))
            if t < NT:
                todo.append(lambda t=t: ffn_up(t))
            if t > 0:
                todo.append(lambda t=t: ffn_out(t - 1))
        side = {}

        def at(r, s, fn, *a):
            side.setdefault((r, s), []).append(lambda: fn(*a))

        for b in range(NB):
            at(0, b + 2, stats2, b)
        at(1, 1, rstd2)
        for b in range(3, NB):
            at(b - 3, 1, rope, b, "gpsimd")
            at(b - 3, 1, residual, b)
        for b, (r, s) in enumerate([(1, 9), (2, 3), (2, 8), (3, 3), (3, 9), (4, 8), (5, 6), (6, 4)]):
            at(r, s, renorm, b)
        for b in range(1, NB):
            r, s = (0, 3) if b == 1 else (b // 2, 2 + 4 * (b % 2))
            at(r, s, router_in, b)
            at(r, s + 2, router, b)
            r = max(4 * b - 4, 1)
            at(r, 1, project_in, b)
            at(r, 3, project, b, "k")
            at(r, 5, project, b, "q")
            at(r, 7, project_v, b)
        at(4, 4, route)
        for k in range(NK):
            at(5 + (4 + k // 2) // 11, (4 + k // 2) % 11, scatter, k)
        at(6, 10, first)
        for b in range(1, NB):
            side.setdefault((max(4 * b - 2, 2), 8), []).append(lambda b=b: operands(b))
        FIRST, LAST = 7, NS + 2
        per = len(todo) / (11 * (LAST - FIRST))
        owed = 0.0
        for r in range(NS + 5):
            mxu = max_units(r) if r < NS else []
            scu = score_units(r - 2) if 0 <= r - 2 < NS else []
            pvu = pv_units(r - 3) if 0 <= r - 3 < NS else []
            for s in range(11):
                tick()
                if s == 1 and 0 <= r - 1 < NS:
                    max_rows(r - 1)
                if s < len(scu):
                    scu[s]()
                if s < len(mxu):
                    mxu[s]()
                if s % 3 == 0 and pvu:
                    pvu[s // 3]()
                if s == 2 and 0 <= r - 4 < NS:
                    heads(r - 4)
                if s == 5 and 0 <= r - 4 < NS and (r - 4) % NG == NG - 1:
                    mix((r - 4) // NG)
                for f in side.get((r, s), []):
                    f()
                if r >= FIRST:
                    owed += per
                    while owed >= 1 and todo:
                        todo.pop(0)()
                        owed -= 1
                        if not todo:
                            for b in range(NB):
                                load_y(b)
            if r < NS:
                max_split(r)
            if not todo and r >= FIRST:
                for b in range(NB):
                    if ("fin", b) not in st and ("acc", b) in st:
                        finish(b)
        while todo or pending:
            tick()
            if todo:
                todo.pop(0)()
                if not todo:
                    for b in range(NB):
                        load_y(b)
        for b in range(NB):
            if ("fin", b) not in st:
                finish(b)
        fl.wait("sync", [st["out"], st["yst", NT - 1], st["yst", NT - 2], st["scat"], zero_x,
                         st["q", 0], st["k", 0]])
        fl.run(ctx.enter_context(nc.Block()))


def kernel(**inputs):
    import concourse.bacc as bacc
    from concourse.bass_utils import run_bass_kernel_spmd

    a = {k[3:]: np.asarray(v) for k, v in inputs.items()}
    f32 = np.float32
    tab = np.zeros((E, P, ROW), f32)
    tab[:, :, C_W1:C_W1 + F] = a["ffn_W1"].transpose(0, 2, 1)
    tab[:, :, C_W2:C_W2 + F] = a["ffn_W2"].transpose(0, 2, 1).reshape(E, 4, P, D).transpose(0, 2, 1, 3).reshape(E, P, F)
    tab[:, :, C_G] = a["ffn_gamma"]
    tab[:, :, C_B] = a["ffn_beta"]
    tab[:, :, C_B1:C_B1 + 4] = a["ffn_b1"].reshape(E, 4, P).transpose(0, 2, 1)
    tab[:, :, C_B2:C_B2 + D] = a["ffn_b2"][:, None, :]
    cst = np.zeros((P, KW), f32)
    p = np.arange(P)
    cst[:, K_ID:K_ID + P] = np.eye(P)
    cst[:, K_MASK + S - P:K_MASK + S] = np.where(p[None, :] > p[:, None], -1e30, 0.0)
    cst[:, K_TRI:K_TRI + P] = p[:, None] < p[None, :]
    cst[:, K_ONE:K_ONE + P] = 1.0
    theta = (f32(1.0) / f32(10000.0) ** (np.arange(64, dtype=f32) / f32(64))).astype(f32)
    ang = np.arange(S, dtype=f32)[:, None] * theta[None, :]
    for k, fn in ((K_COS, np.cos), (K_SIN, np.sin)):
        cst[:, k:k + 256] = fn(ang).astype(f32).reshape(NI, P, 64).transpose(1, 0, 2).reshape(P, 256)
    cst[:, K_IE:K_IE + E] = np.arange(E)
    cst[:, K_IE8:K_IE8 + E] = np.arange(E) + 8
    cst[:, K_J:K_J + 32] = np.arange(32) * P
    cst[:, K_T:K_T + NT] = np.arange(NT)
    cst[:, K_P] = p
    cst[:, K_TOK:K_TOK + NK] = np.arange(NK)[None, :] * P + p[:, None]
    arrays = {
        "X": a["attn_X"],
        "wq": a["attn_W_q"].T,
        "wkv": np.concatenate([a["attn_W_k"], a["attn_W_v"]]).T,
        "wo": a["attn_W_o"].T,
        "cen": a["ffn_centroids"].T,
        "tab": tab.reshape(E * P, ROW),
        "cst": cst,
    }
    arrays = {"in_" + k: np.ascontiguousarray(v) for k, v in arrays.items()}
    nc = bacc.Bacc("TRN2", target_bir_lowering=False, num_devices=1)
    args = [nc.dram_tensor(k, v.shape, mybir.dt.from_np(v.dtype), kind="ExternalInput").ap() for k, v in arrays.items()]
    out = nc.dram_tensor("out", (NB, S, D), F32, kind="ExternalOutput").ap()
    build(nc, *args, out)
    r = run_bass_kernel_spmd(nc, [arrays], core_ids=[0])
    return r.results[0]["out"]
```

```python
from contextlib import ExitStack

import numpy as np

import concourse.bass as bass
from concourse import mybir

F32 = mybir.dt.float32
BF16 = mybir.dt.bfloat16
I32 = mybir.dt.int32
ALU = mybir.AluOpType
ACT = mybir.ActivationFunctionType
AX = mybir.AxisListType.X

P = 128
NB = 8
NI = 4
NK = NB * NI
S = 512
D = 128
NH = 16
NG = 4
E = 8
F = 512
EPS = 1e-5
SCALE = 1.0 / float(np.sqrt(np.float32(8)))
NT = (NK * P + E * (P - 1)) // P
ROW = 1168
C_W1, C_W2, C_G, C_B, C_B1, C_B2 = 0, 512, 1024, 1025, 1026, 1040
K_ID, K_TRI, K_ONE, K_COS, K_SIN, K_MASK = 0, 128, 256, 512, 768, 1177
K_IE, K_IE8, K_J, K_T, K_P, K_Z, K_TOK = 1024, 1032, 1040, 1072, 1112, 1113, 1145
K_LOW = 1177 + 512
KW = K_LOW + 128
XW = D + 4
C_TOK, C_RS, C_NB = D, D + 1, D + 2
NY = NK * P + NT * P
MROW = 96


class Flow:

    ENGINES = ("sync", "gpsimd", "scalar", "tensor", "vector")

    def __init__(self, nc, ctx):
        self.nc, self.ctx = nc, ctx
        self.queue = {e: [] for e in self.ENGINES}
        self.count, self.sems = {}, {}
        self.waited = {e: {} for e in self.ENGINES}

    def mark(self, sem, step):
        if sem not in self.sems:
            self.sems[sem] = self.ctx.enter_context(self.nc.semaphore(sem))
            self.count[sem] = 0
        self.count[sem] += step
        return sem, self.count[sem]

    def wait(self, eng, after):
        for m in after:
            if m is not None and self.waited[eng].get(m[0], 0) < m[1]:
                self.waited[eng][m[0]] = m[1]
                self.queue[eng].append(lambda e, s=self.sems[m[0]], v=m[1]: e.wait_ge(s, v))

    def do(self, eng, fn, after=(), sem=None, step=1):
        self.wait(eng, after)
        if sem is None:
            self.queue[eng].append(fn)
            return None
        m = self.mark(sem, step)
        self.queue[eng].append(lambda e, s=self.sems[sem]: fn(e).then_inc(s, step))
        return m

    def dma(self, eng, fn, after=(), sem=None):
        return self.do(eng, fn, after, sem, 16)

    def run(self, block):
        for name in self.ENGINES:
            def body(e, q=self.queue[name]):
                for f in q:
                    f(e)
            (block.sync if name == "sync" else block.gpsimd if name == "gpsimd" else block.scalar if name == "scalar"
             else block.tensor if name == "tensor" else block.vector)(body)


def build(nc, X_d, wq_d, wkv_d, wo_d, cen_d, tab_d, cst_d, pad_d, blank_d, out_d):
    with ExitStack() as ctx:
        fl = Flow(nc, ctx)
        do, dma = fl.do, fl.dma

        def sb(name, shape, dt=F32):
            return ctx.enter_context(nc.sbuf_tensor(name, shape, dt))

        def ps(name, shape, dt=F32):
            return ctx.enter_context(nc.psum_tensor(name, shape, dt))

        def dram(name, shape, dt=F32):
            return nc.dram_tensor(name, shape, dt, kind="Internal").ap()

        xs_d = dram("xs_d", (NT * P, XW))
        ys_d = dram("ys_d", (NY, D))
        od = [dram(f"od{b}", (NG, P, S)) for b in range(NB)]
        rd = [dram(f"rd{b}", (P, 64)) for b in range(NB)]
        qd = [dram(f"qd{b}", (3, P, S), BF16) for b in range(NB)]
        kd = [dram(f"kd{b}", (3, 32, S), BF16) for b in range(NB)]

        cst = sb("cst", [P, KW])
        idf = cst[:, K_ID:K_ID + P]
        idb = sb("idb", [P, P], BF16)
        trib = sb("trib", [P, P], BF16)
        oneb = sb("oneb", [P, P], BF16)
        lowb = sb("lowb", [P, P], BF16)
        cosT = cst[:, K_COS:K_COS + 256].rearrange("p (i c) -> p i c", i=NI)
        sinT = cst[:, K_SIN:K_SIN + 256].rearrange("p (i c) -> p i c", i=NI)
        wq = sb("wq", [P, P])
        wkv = sb("wkv", [P, 64])
        wo = sb("wo", [P, P])
        cen = sb("cen", [P, E])
        X = sb("X", [P, NK, D])
        xh = sb("xh", [P, NK, XW])
        xr = sb("xr", [P, NK, D])
        rt = sb("rt", [P, NI, 64])
        xnT = sb("xnT", [P, S])
        xrT = sb("xrT", [P, S])
        qp = sb("qp", [P, 3, S], BF16)
        kp = sb("kp", [P, 3, P], BF16)
        qr = sb("qr", [P, S])
        kr = sb("kr", [P, P])
        Qop = sb("Qop", [P, 2, NH, S], BF16)
        Kop = sb("Kop", [P, 2, NG, S], BF16)
        V = sb("V", [P, 3 * NI, NG, 32])
        PT = [sb(f"PT{i}", [P, 4 * 1280]) for i in range(2)]
        st1 = sb("st1", [P, NK, 6])
        mv1 = sb("mv1", [P, NK, 2])
        sm2, nm2, sq2 = (sb(n, [P, NK]) for n in ("sm2", "nm2", "sq2"))
        junk = sb("junk", [P, NI, D])
        rs1, nb1, rp1 = (sb(n, [P, NK]) for n in ("rs1", "nb1", "rp1"))
        mx = sb("mx", [P, 2, 4, NI])
        nm = sb("nm", [P, 2, 2, 4, NI], BF16)
        mT = sb("mT", [32, 2, P], BF16)
        O = sb("O", [P, 2, S])
        den = sb("den", [P, S])
        rc = sb("rc", [P, 64])
        att = sb("att", [P, NI, D])
        rden = sb("rden", [P, NI, 4])
        attT = sb("attT", [P, 2, S])
        wt = [sb(f"wt{i}", [P, ROW])[:, :] for i in range(3)]
        xt = [sb(f"xt{i}", [P, XW])[:, :] for i in range(3)]
        tid = sb("tid", [P, 3], I32)
        hT = sb("hT", [P, 2, P])
        h1 = sb("h1", [P, 2, 4, P])
        yt = sb("yt", [P, 2, D])
        sc = sb("sc", [P, NK, E])
        smx, sam, alpha, ea = (sb(n, [P, NK]) for n in ("smx", "sam", "alpha", "ea"))
        eq, oh, tot, incl = (sb(n, [P, NK, E]) for n in ("eq", "oh", "tot", "incl"))
        ohb = sb("ohb", [P, NK, E], BF16)
        cmpn = sb("cmpn", [P, E, 32])
        ntl, tend, tst = (sb(n, [P, E]) for n in ("ntl", "tend", "tst"))
        cmpt = sb("cmpt", [P, NT, E])
        et = sb("et", [P, NT])
        posf = sb("posf", [P, NK])
        posi = sb("posi", [P, NK], I32)
        widx = sb("widx", [P, NT], I32)

        MX = [ps(f"MX{i}", [P, 512]) for i in range(2)]
        SC = [ps(f"SC{i}", [P, 512]) for i in range(2)]
        PV = ps("PV", [P, 512])
        MI = [ps(f"MI{i}", [P, 512]) for i in range(3)]

        banks = {"next": 0, "free": [[], [], []], "held": [False] * 3}
        pending = []
        clock = [0]

        def later(slots, fn):
            if clock[0] == 0:
                fn()
            else:
                pending.append((clock[0] + slots, len(pending), fn))

        def tick():
            clock[0] += 1
            while any(p[0] <= clock[0] for p in pending):
                first_pending()

        def first_pending():
            p = min(pending, key=lambda x: x[0])
            pending.remove(p)
            p[2]()

        def misc():
            k = banks["next"] % 3
            banks["next"] += 1
            while banks["held"][k]:
                first_pending()
            banks["held"][k] = True
            return k

        def release(k, mark):
            banks["held"][k] = False
            banks["free"][k] = [mark]

        mi_free = banks["free"]

        def spread(steps):
            if next(steps, True) is None:
                later(1, lambda: spread(steps))

        def load_x(b):
            return dma("sync", lambda e: e.dma_start(
                X[:, NI * b:NI * b + NI, :], X_d[b].rearrange("(i p) d -> p i d", p=P)), sem=f"l_x{b}")

        def load_pad(u):
            dma("sync", lambda e: e.dma_start(
                Kop[72:P, u, :, :].bitcast(F32).rearrange("p g s -> p (g s)"), pad_d[:, 0:1024]), sem=f"pad{u}")
            return dma("sync", lambda e: e.dma_start(
                Qop[72:P, u, :, :].bitcast(F32).rearrange("p h s -> p (h s)"), pad_d[:, 1024:5120]), sem=f"pad{u}")

        x_in = [load_x(0)]
        l_c = dma("sync", lambda e: e.dma_start(cst[:, :], cst_d), sem="l_cst")
        for t, s in ((wkv, wkv_d), (wq, wq_d), (cen, cen_d), (wo, wo_d)):
            l_w = dma("sync", lambda e, t=t, s=s: e.dma_start(t[:, :], s), sem="l_w")
        x_in += [load_x(b) for b in range(1, NB)]
        pads = [load_pad(0)]
        z_v = do("gpsimd", lambda e: e.memset(V[:, :, :, :], 1.0), sem="clr")
        do("gpsimd", lambda e: e.memset(xh[:, :, D + 3], 0.0), sem="clr")
        z_tok = do("gpsimd", lambda e: e.tensor_copy(xh[:, :, C_TOK], cst[:, K_TOK:K_TOK + NK]), [l_c], sem="clr")

        st = {}

        def stats(b):
            ks = range(NI * b, NI * b + NI)
            for k in ks:
                a = do("vector", lambda e, k=k: e.bn_stats(st1[:, k, :], X[:, k, :]), [x_in[b]], "v_ln")
            for k in ks:
                st["mv"] = do("vector", lambda e, k=k: e.bn_aggr(mv1[:, k, :], st1[:, k, :]), [a], "v_ln")

        def squares(b):
            ks = slice(NI * b, NI * b + NI)
            a = st["n", b]
            if b == 0:
                a = do("vector", lambda e: e.tensor_reduce(sm2[:, ks], xh[:, ks, 0:D], AX, ALU.add), [a], "v_ln")
            a = do("vector", lambda e: e.tensor_scalar(nm2[:, ks], sm2[:, ks], -1.0 / D, None, ALU.mult), [a], "v_ln")

            def read():
                done = st.get("sq")
                for k in range(NI * b, NI * b + NI):
                    st["sq"] = do("scalar", lambda e, k=k: e.activation(
                        junk[:, k % NI, :], xh[:, k, 0:D], ACT.Square, bias=nm2[:, k:k + 1], accum_out=sq2[:, k:k + 1]),
                        [a, done], "a_sq")
            later(1, read)

        def invert(b0, b1):
            ks = slice(NI * b0, NI * b1)
            r = rs1[:, ks]
            a = do("vector", lambda e: e.tensor_scalar(r, mv1[:, ks, 1], EPS, None, ALU.add), [st["mv"]], "v_ln")
            a = do("scalar", lambda e: e.activation(r, r, ACT.Sqrt), [a], "a_ln")
            a = st["rs0"] = do("vector", lambda e: e.reciprocal(r, r), [a], "v_ln")
            do("vector", lambda e: e.scalar_tensor_tensor(
                out=nb1[:, ks], in0=mv1[:, ks, 0], scalar=-1.0, in1=r, op0=ALU.mult, op1=ALU.mult), [a], "v_ln")
            a = do("vector", lambda e: e.tensor_scalar(rp1[:, ks], r, 1.0, None, ALU.add), [a], "v_ln")
            for b in range(b0, b1):
                st["rs", b] = a

        def invert2():
            r = xh[:, :, C_RS]
            a = do("vector", lambda e: e.tensor_scalar(r, sq2[:, :], 1.0 / D, EPS, ALU.mult, ALU.add), [st["sq"]],
                   "v_ln")
            a = do("scalar", lambda e: e.activation(r, r, ACT.Sqrt), [a], "a_ln")
            a = do("vector", lambda e: e.reciprocal(r, r), [a], "v_ln")
            st["rs2"] = do("vector", lambda e: e.tensor_tensor(xh[:, :, C_NB], nm2[:, :], r, ALU.mult), [a], "v_ln")

        def norm(b):
            if b:
                for k in range(NI * b, NI * b + NI):
                    st["n", b] = do("scalar", lambda e, k=k: e.activation(
                        xh[:, k, 0:D], X[:, k, :], ACT.Identity, bias=nb1[:, k:k + 1], scale=rs1[:, k:k + 1],
                        accum_out=sm2[:, k:k + 1]), [st["rs", b]], "a_xn")
                return
            for k in range(NI):
                st["n", b] = do("vector", lambda e, k=k: e.tensor_scalar(
                    xh[:, k, 0:D], X[:, k, :], mv1[:, k, 0:1], rs1[:, k:k + 1], ALU.subtract, ALU.mult),
                    [st["rs0"]], "v_ln")

        def residual(k):
            st["xs", k // NI] = do("scalar", lambda e: e.activation(
                X[:, k, :], X[:, k, :], ACT.Identity, bias=nb1[:, k:k + 1], scale=rp1[:, k:k + 1]),
                [st["rs", k // NI], st["n", k // NI]], "a_xs")

        def router_in(b):
            k0, m = NI * b, misc()
            for i in range(NI):
                t = do("tensor", lambda e, i=i: e.transpose(MI[m][:, i * P:i * P + P], xh[:, k0 + i, 0:D], idf),
                       [l_c, st["n", b]] + mi_free[m], "p_xnT")
            st["xnTp", b] = t

            def read():
                st["xnTc"] = do("scalar", lambda e: e.activation(xnT[:, :], MI[m][:, :], ACT.Copy),
                                [t, st.get("xnT")], "a_xnT")
                release(m, st["xnTc"])
            later(1, read)

        def router(b):
            k0, m = NI * b, misc()
            for i in range(NI):
                t = do("tensor", lambda e, i=i: e.matmul(MI[m][:, i * E:i * E + E], xnT[:, i * P:i * P + P],
                                                         cen[:, :], start=True, stop=True),
                       [st["xnTc"], l_w] + mi_free[m], "p_sc")
            st["xnT"] = t

            def read():
                st["sc"] = do("vector", lambda e: e.tensor_copy(
                    sc[:, k0:k0 + NI, :], MI[m][:, 0:NI * E].rearrange("p (i c) -> p i c", i=NI)), [t], "v_sc")
                release(m, st["sc"])
            later(1, read)

        def rope(b, eng):
            v = xh[:, NI * b:NI * b + NI, 0:D].rearrange("p i (c two) -> p i c two", two=2)
            xe, xo = v[:, :, :, 0], v[:, :, :, 1]
            lo, hi = xr[:, NI * b:NI * b + NI, 0:64], xr[:, NI * b:NI * b + NI, 64:128]
            sem = "v_rope" if eng == "vector" else "g_rope"
            w = [st["n", b], l_c, st.get("rt")]
            do(eng, lambda e: e.tensor_tensor(lo, xe, cosT, ALU.mult), w, sem)
            a = do(eng, lambda e: e.tensor_tensor(rt[:, :, :], xo, sinT, ALU.mult), w, sem)
            a = do(eng, lambda e: e.tensor_tensor(lo, lo, rt[:, :, :], ALU.subtract), [a], sem)
            do(eng, lambda e: e.tensor_tensor(hi, xe, sinT, ALU.mult), sem=sem)
            a = do(eng, lambda e: e.tensor_tensor(rt[:, :, :], xo, cosT, ALU.mult), [a], sem)
            a = do(eng, lambda e: e.tensor_tensor(hi, hi, rt[:, :, :], ALU.add), [a], sem)
            st["r", b] = st["rt"] = a

        def project_in(b):
            m = misc()
            for i in range(NI):
                t = do("tensor", lambda e, i=i: e.transpose(MI[m][:, i * P:i * P + P], xr[:, NI * b + i, :], idf),
                       [l_c, st["r", b]] + mi_free[m], "p_xrT")
            st["xrTp", b] = t

            def read():
                st["xrTc"] = do("scalar", lambda e: e.activation(xrT[:, :], MI[m][:, :], ACT.Copy),
                                [t, st.get("xrT")], "a_xrT")
                release(m, st["xrTc"])
            later(1, read)

        def project_v(b):
            k0, m = NI * (b % 3), misc()
            for i in range(NI):
                t = do("tensor", lambda e, i=i: e.matmul(MI[m][:, i * 32:i * 32 + 32], xrT[:, i * P:i * P + P],
                                                         wkv[:, 32:64], start=True, stop=True),
                       [st["xrTc"], l_w] + mi_free[m], "p_q")
            st["xrT"] = t

            def read():
                st["V", b] = do("vector", lambda e: e.tensor_copy(
                    V[:, k0:k0 + NI, :, 0:8], MI[m][:, 0:P].rearrange("p (i g d) -> p i g d", i=NI, g=NG)),
                    [t, z_v, st.get(("pv", 4 * b - 9))], "v_v")
                release(m, st["V", b])
            later(1, read)

        def project(b, key):
            m = misc()
            part, rem, n = (qp, qr, S) if key == "q" else (kp, kr, P)
            src = MI[m][:, 0:n]
            if key == "q":
                t = do("tensor", lambda e: e.matmul(src, wq[:, :], xrT[:, :], start=True, stop=True),
                       [st["xrTc"], l_w] + mi_free[m], "p_q")
            else:
                for c in range(NI):
                    t = do("tensor", lambda e, c=c: e.matmul(
                        MI[m][32 * c:32 * c + 32, 0:P], wkv[:, 0:32], xrT[:, c * P:c * P + P], start=True, stop=True),
                        [st["xrTc"], l_w] + mi_free[m], "p_q")
            st["xrT"] = t

            def part0():
                a = do("scalar", lambda e: e.activation(part[:, 0, :], src, ACT.Copy),
                       [t, st.get(key)] + (q0 if b == 1 else []), "a_sp")
                if key == "q" and b == 0:
                    first_q(0, a)
                later(1, lambda: rest1(a))

            def rest1(a):
                v = do("vector", lambda e: e.tensor_tensor(rem[:, :], src, part[:, 0, :], ALU.subtract),
                       [a, st.get((key, "r"))], "v_sp")
                release(m, v)
                later(1, lambda: part1(v))

            def part1(v):
                a = do("scalar", lambda e: e.activation(part[:, 1, :], rem[:, :], ACT.Copy), [v], "a_sp")
                if key == "q" and b == 0:
                    first_q(1, a)
                later(1, lambda: part2(a))

            def part2(a):
                v = do("vector", lambda e: e.tensor_tensor(part[:, 2, :], rem[:, :], part[:, 1, :], ALU.subtract),
                       [a], "v_sp")
                st[key, "r"] = v
                if key == "q" and b == 0:
                    first_q(2, v)
                elif key == "q":
                    st[key] = dma("sync", lambda e: e.dma_start(qd[b].rearrange("a n t -> n a t"), qp[:, :, :]), [v],
                                  "st_q")
                else:
                    for c in range(NI):
                        st[key] = dma("sync", lambda e, c=c: e.dma_start(
                            kd[b].rearrange("a n t -> n a t")[:, :, c * P:c * P + P], kp[32 * c:32 * c + 32, :, :]),
                            [v], "st_k")
            later(1, part0)

        def first_q(a, after):
            for j in range(3):
                st["q", a] = dma("sync" if a else "gpsimd", lambda e, j=j: e.dma_start(
                    Qop[24 * j + 8 * a:24 * j + 8 * a + 8, 0, :, :], qp[:, a, :]), [after], f"ld_q{a}")

        def operands(b):
            u = b % 2
            free = [pads[u]] + [st.get(("scored", b - 2, g)) for g in range(NG)]
            k = kd[b].rearrange("a (d g) t -> (a d) (g t)", d=8)
            q = qd[b].rearrange("a (d h) t -> (a d) (h t)", d=8)
            ko = Kop[:, u, :, :].rearrange("p g t -> p (g t)")
            qo = Qop[:, u, :, :].rearrange("p h t -> p (h t)")
            for j in range(3):
                for o, i, n in ((24 * j, 8 * j, 24 - 8 * j), (24 * j + 24 - 8 * j, 0, 8 * j)):
                    if n:
                        st["op", b] = dma("sync" if b else "scalar", lambda e, o=o, i=i, n=n: e.dma_start(
                            ko[o:o + n, :], k[i:i + n, :]), [st["k"]] + free, f"ld_op{u}")
                if b:
                    st["op", b] = dma("sync", lambda e, j=j: e.dma_start(qo[24 * j:24 * j + 24, :], q),
                                      [st["q"]] + free, f"ld_op{u}")

        def route():
            seq = lambda fn, after=(), eng="vector": do(eng, fn, list(after), "v_rt")
            bc = lambda a: a.unsqueeze(2).to_broadcast([P, NK, E])
            kc = lambda o, n: cst[:, o:o + n]
            a = seq(lambda e: e.tensor_reduce(smx[:, :], sc[:, :, :], AX, ALU.max), [st["sc"], l_c])
            x = do("scalar", lambda e: e.activation(ea[:, :], smx[:, :], ACT.Exp, scale=-1.0), [a], "a_al")
            a = seq(lambda e: e.tensor_tensor(eq[:, :, :], sc[:, :, :], bc(smx[:, :]), ALU.is_equal), [a])
            yield
            a = seq(lambda e: e.scalar_tensor_tensor(
                out=eq[:, :, :], in0=eq[:, :, :], scalar=-8.0,
                in1=kc(K_IE8, E).unsqueeze(1).to_broadcast([P, NK, E]), op0=ALU.mult, op1=ALU.add), [a])
            a = seq(lambda e: e.tensor_reduce(sam[:, :], eq[:, :, :], AX, ALU.min), [a])
            yield
            a = seq(lambda e: e.tensor_tensor(oh[:, :, :], kc(K_IE, E).unsqueeze(1).to_broadcast([P, NK, E]),
                                              bc(sam[:, :]), ALU.is_equal), [a])
            a = seq(lambda e: e.tensor_copy(ohb[:, :, :], oh[:, :, :]), [a])
            yield
            m = misc()
            flat = ohb[:, :, :].rearrange("p k c -> p (k c)")
            do("tensor", lambda e: e.matmul(MI[m][:, 0:256], trib[:, :], flat, start=True, stop=True),
               [a, consts] + mi_free[m], "p_rt")
            t = do("tensor", lambda e: e.matmul(MI[m][:, 256:512], oneb[:, :], flat, start=True, stop=True),
                   sem="p_rt")
            yield
            a = seq(lambda e: e.tensor_scalar(ea[:, :], ea[:, :], 1.0, None, ALU.add), [x])
            st["alpha"] = seq(lambda e: e.reciprocal(alpha[:, :], ea[:, :]), [a])
            a = seq(lambda e: e.tensor_copy(tot[:, :, :], MI[m][:, 256:512].rearrange("p (k c) -> p k c", c=E)), [t])
            yield
            for c in range(E):
                a2 = seq(lambda e, c=c: e.tensor_tensor_scan(incl[:, :, c], tot[:, :, c], kc(K_Z, NK), 0.0, ALU.add,
                                                             ALU.add), [a])
            yield
            a = seq(lambda e: e.tensor_tensor(
                cmpn[:, :, :], incl[:, NK - 1, :].unsqueeze(2).to_broadcast([P, E, 32]),
                kc(K_J, 32).unsqueeze(1).to_broadcast([P, E, 32]), ALU.is_gt), [a2])
            a = seq(lambda e: e.tensor_reduce(ntl[:, :], cmpn[:, :, :], AX, ALU.add), [a])
            yield
            a = seq(lambda e: e.tensor_tensor_scan(tend[:, :], ntl[:, :], kc(K_Z, E), 0.0, ALU.add, ALU.add), [a])
            a3 = seq(lambda e: e.tensor_tensor(tst[:, :], tend[:, :], ntl[:, :], ALU.subtract), [a])
            a = seq(lambda e: e.tensor_tensor(incl[:, :, :], incl[:, :, :], tot[:, :, :], ALU.subtract), [a2])
            yield
            a = seq(lambda e: e.scalar_tensor_tensor(
                out=incl[:, :, :], in0=tst[:, :].unsqueeze(1).to_broadcast([P, NK, E]), scalar=float(P),
                in1=incl[:, :, :], op0=ALU.mult, op1=ALU.add), [a, a3])
            a = seq(lambda e: e.tensor_tensor(incl[:, :, :], MI[m][:, 0:256].rearrange("p (k c) -> p k c", c=E),
                                              incl[:, :, :], ALU.add), [a])
            release(m, a)
            yield
            a = seq(lambda e: e.tensor_tensor(incl[:, :, :], incl[:, :, :], oh[:, :, :], ALU.mult), [a])
            a = seq(lambda e: e.tensor_reduce(posf[:, :], incl[:, :, :], AX, ALU.add), [a])
            yield
            st["pos"] = seq(lambda e: e.tensor_copy(posi[:, :], posf[:, :]), [a])
            a = seq(lambda e: e.tensor_tensor(
                cmpt[:, :, :], kc(K_T, NT).unsqueeze(2).to_broadcast([P, NT, E]),
                tend[:, :].unsqueeze(1).to_broadcast([P, NT, E]), ALU.is_ge), [a3])
            yield
            a = seq(lambda e: e.tensor_reduce(et[:, :], cmpt[:, :, :], AX, ALU.add), [a])
            a = seq(lambda e: e.tensor_scalar(et[:, :], et[:, :], float(E - 1), float(P), ALU.min, ALU.mult), [a])
            a = seq(lambda e: e.tensor_scalar(et[:, :], et[:, :], kc(K_P, 1), None, ALU.add), [a])
            st["widx"] = seq(lambda e: e.tensor_copy(widx[:, :], et[:, :]), [a])

        def weights(t):
            st["wt", t] = dma("gpsimd", lambda e: e.indirect_dma_start(
                out=wt[t % 3], out_offset=None, in_=tab_d,
                in_offset=bass.IndirectOffsetOnAxis(ap=widx[:, t:t + 1], axis=0)),
                [st["widx"], st.get(("y", t - 3))], f"ld_wt{t % 3}")

        def scatter(k):
            st["scat"] = dma("gpsimd", lambda e: e.indirect_dma_start(
                out=xs_d, out_offset=bass.IndirectOffsetOnAxis(ap=posi[:, k:k + 1], axis=0),
                in_=xh[:, k, :], in_offset=None),
                [st["pos"], zero_x, z_tok, st["rs2"]], "scat")

        def load_tile(t):
            st["xt", t] = dma("sync", lambda e: e.dma_start(xt[t % 3], xs_d[t * P:t * P + P, :]),
                              [st["scat"], st.get(("xT", t - 3)), st.get(("tid", t - 3))], f"ld_xt{t % 3}")

        def ffn_norm(t):
            x = xt[t % 3]
            st["xn", t] = do("scalar", lambda e: e.activation(
                x[:, 0:D], x[:, 0:D], ACT.Identity, bias=x[:, C_NB:C_NB + 1], scale=x[:, C_RS:C_RS + 1]),
                [st["xt", t]], "a_xt")

        def ffn_in(t):
            m = misc()
            p = do("tensor", lambda e: e.transpose(MI[m][:, 0:P], xt[t % 3][:, 0:D], idf), [st["xn", t]] + mi_free[m],
                   "p_xT")
            st["xT", t] = p
            w = wt[t % 3]

            def read():
                st["hT", t] = do("vector", lambda e: e.tensor_scalar(
                    hT[:, t % 2, :], MI[m][:, 0:P], w[:, C_G:C_G + 1], w[:, C_B:C_B + 1], ALU.mult, ALU.add),
                    [p, st["wt", t], st.get(("h", t - 2, "mm"))], "v_hT")
                release(m, st["hT", t])
                st["tid", t] = do("vector", lambda e: e.tensor_copy(
                    tid[:, t % 3:t % 3 + 1], xt[t % 3][:, C_TOK:C_TOK + 1]), [st["xt", t], st.get(("yst", t - 3))], "v_tid")
                if t + 3 < NT:
                    load_tile(t + 3)
            later(1, read)

        def ffn_up(t, half):
            w = wt[t % 3]
            if half == 0:
                st["up", t] = misc()
            m = st["up", t]
            for c in (2 * half, 2 * half + 1):
                p = do("tensor", lambda e, c=c: e.matmul(
                    MI[m][:, c * P:c * P + P], w[:, C_W1 + c * P:C_W1 + c * P + P], hT[:, t % 2, :],
                    start=True, stop=True), [st["hT", t], st["wt", t]] + mi_free[m], "p_h")
            if half == 0:
                return
            st["h", t, "mm"] = p

            def read(c0):
                for c in (c0, c0 + 1):
                    a = do("scalar", lambda e, c=c: e.activation(
                        h1[:, t % 2, c, :], MI[m][:, c * P:c * P + P], ACT.Relu, bias=w[:, C_B1 + c:C_B1 + c + 1]),
                        [p, st.get(("ymm", t - 2))], "a_h")
                st["hh", t, c0] = a
                if c0 == 0:
                    later(1, lambda: read(2))
                else:
                    release(m, a)
            later(1, lambda: read(0))

        def ffn_down(t, half):
            w = wt[t % 3]
            if half == 0:
                st["down", t] = misc()
            m = st["down", t]
            for c in (2 * half, 2 * half + 1):
                p = do("tensor", lambda e, c=c: e.matmul(
                    MI[m][:, 0:D], h1[:, t % 2, c, :], w[:, C_W2 + c * P:C_W2 + c * P + P], start=(c == 0),
                    stop=(c == 3)), [st["hh", t, c // 2 * 2]] + mi_free[m], "p_y")
            if half == 0:
                return
            st["ymm", t] = p

            def read():
                st["y", t] = do("vector", lambda e: e.tensor_tensor(
                    yt[:, t % 2, :], MI[m][:, 0:D], w[:, C_B2:C_B2 + D], ALU.add),
                    [p, st.get(("yst", t - 2))], "v_y")
                release(m, st["y", t])
            later(1, read)

        def ffn_out(t):
            st["yst", t] = dma("gpsimd", lambda e: e.indirect_dma_start(
                out=ys_d, out_offset=bass.IndirectOffsetOnAxis(ap=tid[:, t % 3:t % 3 + 1], axis=0),
                in_=yt[:, t % 2, :], in_offset=None), [st["y", t], st["tid", t]], f"st_y{t % 2}")
            if t + 3 < NT:
                weights(t + 3)

        mxn, scn = [0], [0]
        mx_free, sc_free = [None, None], [None, None]

        def max_units(n):
            b, g = n // NG, n % NG
            u, q = b % 2, n % 2
            def unit(i, hs):
                def emit():
                    k = mxn[0] % 2
                    mxn[0] += 1
                    w = (i + 1) * P
                    for j, h in enumerate(hs):
                        t = do("tensor", lambda e, j=j, h=h: e.matmul(
                            MX[k][:, j * w:j * w + w], Qop[0:MROW, u, 4 * g + h, i * P:i * P + P],
                            Kop[0:MROW, u, g, 0:w], start=True, stop=True), [st["op", b], pads[u], mx_free[k]] + (q0 if b == 0 else []), "p_mx")
                    for j, h in enumerate(hs):
                        a = do("vector", lambda e, j=j, h=h: e.tensor_tensor_reduce(
                            MX[k][:, j * w:j * w + w], MX[k][:, j * w:j * w + w], cst[:, K_MASK + S - w:K_MASK + S], 1.0, -3e38,
                            ALU.add, ALU.max, mx[:, q, h, i:i + 1]), [t, st.get(("nm", n - 2))], "v_mx")
                    mx_free[k] = st["mx", n] = a
                return emit
            return ([unit(3, [h]) for h in range(4)] + [unit(2, [h]) for h in range(4)]
                    + [unit(1, [0, 1]), unit(1, [2, 3]), unit(0, [0, 1, 2, 3])])

        def max_split(n):
            q = n % 2
            a = do("vector", lambda e: e.tensor_scalar(nm[:, q, 0, :, :], mx[:, q, :, :], -1.0, None, ALU.mult),
                   [st["mx", n], st.get(("mTp", n - 2))], "v_nm")
            st["nm", n] = do("vector", lambda e: e.scalar_tensor_tensor(
                out=nm[:, q, 1, :, :], in0=mx[:, q, :, :], scalar=-1.0, in1=nm[:, q, 0, :, :], op0=ALU.mult,
                op1=ALU.subtract), [a], "v_nm")

        def max_rows(n):
            b, g = n // NG, n % NG
            u, q, m = b % 2, n % 2, misc()
            pt = MI[m][:, :].bitcast(BF16)
            t = st["mTp", n] = do("tensor", lambda e: e.transpose(
                pt[0:32, 0:P], nm[:, q, :, :, :].rearrange("p a h i -> p (a h i)"), idb[:, :]),
                [st["nm", n], consts] + mi_free[m], "p_mT")

            def read():
                a = do("scalar", lambda e: e.activation(mT[:, q, :], pt[0:32, 0:P], ACT.Copy),
                       [t, st.get(("m", n - 2))], "a_mT")
                release(m, a)
                st["m", n] = dma("sync", lambda e: e.dma_start(
                    Qop[MROW:MROW + 2, u, 4 * g:4 * g + 4, :].rearrange("p h (i s) -> p (h i) s", s=P), mT[:, q, :]),
                    [a, st.get(("scored", b - 2, g)), pads[u]], f"ld_m{q}")
            later(1, read)

        OFF = [0, 2048, 2048 + 1536, 2048 + 1536 + 1024]

        def add_mask(n):
            return M0 <= n < M1

        def score_units(n):
            b, g = n // NG, n % NG
            u, q = b % 2, n % 2
            def unit(j, hs, last):
                def emit():
                    k = scn[0] % 2
                    scn[0] += 1
                    w = S - j * P
                    o = OFF[j] + hs[0] * w
                    out = SC[k][:, 0:w * len(hs)].rearrange("p (h s) -> p h s", s=w)
                    t = do("tensor", lambda e: e.matmul(
                        out, Kop[:, u, g, j * P:j * P + P], Qop[:, u, 4 * g + hs[0]:4 * g + hs[0] + len(hs), j * P:S],
                        start=True, stop=not add_mask(n), skip_group_check=add_mask(n)),
                        [st["m", n], st["op", b], sc_free[k]], "p_sc2")
                    if add_mask(n):
                        t = do("tensor", lambda e: e.matmul(
                            out[:, :, 0:P], idb[:, :], lowb[:, :].unsqueeze(1).to_broadcast([P, len(hs), P]),
                            start=False, stop=True, skip_group_check=True), [consts], "p_sc2")
                    st["scored", b, g] = t
                    sc_free[k] = do("scalar", lambda e: e.activation(
                        PT[q][:, o:o + w * len(hs)], SC[k][:, 0:w * len(hs)], ACT.Exp, scale=SCALE),
                        [t, st.get(("pv", n - 2))], "a_ex")
                    if last and add_mask(n):
                        st["P", n, j] = sc_free[k]
                    elif last:
                        blk = PT[q][:, OFF[j]:OFF[j] + 4 * w].rearrange("p (h s) -> p h s", s=w)[:, :, 0:P]
                        st["P", n, j] = do("gpsimd", lambda e: e.affine_select(
                            out=blk, in_=blk, compare_op=ALU.is_ge, fill=0.0, base=0,
                            pattern=[[0, 4], [1, P]], channel_multiplier=-1), [sc_free[k]], "g_mask")
                return emit
            return ([unit(0, [h], h == 3) for h in range(4)] + [unit(1, [h], h == 3) for h in range(4)]
                    + [unit(2, [0, 1], False), unit(2, [2, 3], True), unit(3, [0, 1, 2, 3], True)])

        def pv_units(n):
            b, g = n // NG, n % NG
            q = n % 2
            def unit(j):
                def emit():
                    w = S - j * P
                    for h in range(4):
                        t = do("tensor", lambda e, h=h: e.matmul(
                            PV[32 * h:32 * h + 32, j * P:S], V[:, NI * (b % 3) + j, g, :],
                            PT[q][:, OFF[j] + h * w:OFF[j] + h * w + w], start=(j == 0), stop=(j == 3),
                            skip_group_check=True),
                            [st["P", n, j], st["V", b], st.get(("O", n - 1))], "p_pv")
                    st["pv", n] = t
                    if j == 3:
                        def read():
                            st["O", n] = do("scalar", lambda e: e.activation(O[:, q, :], PV[:, :], ACT.Copy),
                                            [t, st.get(("Ot", n - 2))], "a_O")
                        later(1, read)
                return emit
            return [unit(j) for j in range(4)]

        def heads(n):
            b, g = n // NG, n % NG
            u = b % 2
            st["Ot", n] = dma("sync", lambda e: e.dma_start(od[b][g], O[:, n % 2, :]), [st["O", n]], f"st_o{n % 2}")
            if g == NG - 1:
                done = [st["Ot", n], st["Ot", n - 1]]
                o = od[b].rearrange("g (h c) s -> (g h) c s", c=32)
                st["rc", b] = dma("sync", lambda e: e.dma_start(
                    rc[:, :], o[:, 8, :].rearrange("k (j t) -> k j t", t=64)), done + [st.get(("rd", b - 1))], "ld_rc")
                st["att", b] = dma("sync", lambda e: e.dma_start(attT[:, u, :], o[:, 0:8, :]),
                                   done + [st.get(("wo", b - 2))], f"ld_att{u}")

        def heads_now(n):
            g, q, m = n % NG, n % 2, misc()
            for i in range(NI):
                t = do("tensor", lambda e, i=i: e.transpose(MI[m][:, i * P:i * P + P], O[:, q, i * P:i * P + P], idf),
                       [st["O", n]] + mi_free[m], "p_Ot")
            st["Ot", n] = t
            v = MI[m][:, :].rearrange("p (i h c) -> p i h c", i=NI, h=4)

            def read():
                r = do("vector", lambda e: e.reciprocal(rden[:, :, :], v[:, :, :, 8]), [t, st.get("att")], "v_rd")
                st["att"] = do("vector", lambda e: e.tensor_tensor(
                    att[:, :, 32 * g:32 * g + 32].rearrange("p i (h d) -> p i h d", h=4), v[:, :, :, 0:8],
                    rden[:, :, :].unsqueeze(3).to_broadcast([P, NI, 4, 8]), ALU.mult), [r], "v_att")
                release(m, st["att"])
            later(1, read)

        def mix_now(b):
            u, m = b % 2, misc()
            for i in range(NI):
                t = do("tensor", lambda e, i=i: e.transpose(MI[m][:, i * P:i * P + P], att[:, i, :], idf),
                       [st["att"]] + mi_free[m], "p_aT")

            def read():
                c = do("scalar", lambda e: e.activation(attT[:, u, :], MI[m][:, :], ACT.Copy),
                       [t, st["wo", b - 2]], "a_aT")
                release(m, c)
                later(1, lambda: product(b, c))
            later(1, read)

        def invert_sums(b):
            r = do("vector", lambda e: e.reciprocal(rc[:, :], rc[:, :]), [st["rc", b]], "v_rd")
            st["rd", b] = dma("sync", lambda e: e.dma_start(rd[b], rc[:, :]), [r], "st_rd")
            src = rd[b].rearrange("(k j) t -> k (j t)", j=8).unsqueeze(1).to_broadcast([NH, 8, S])
            st["den", b] = dma("sync", lambda e: e.dma_start(den[:, :], src), [st["rd", b], st.get(("attn", b - 1))],
                               "ld_den")

        def mix(b):
            u = b % 2
            c = st["attn", b] = do("vector", lambda e: e.tensor_tensor(
                attT[:, u, :], attT[:, u, :], den[:, :], ALU.mult), [st["att", b], st["den", b]], "v_att")
            later(4, lambda: product(b, c))

        def product(b, c):
            u, m = b % 2, misc()
            for i in range(NI):
                t = do("tensor", lambda e, i=i: e.matmul(MI[m][:, i * P:i * P + P], attT[:, u, i * P:i * P + P],
                                                         wo[:, :], start=True, stop=True),
                       [c, l_w] + mi_free[m], "p_wo")
            st["wo", b] = t

            def add():
                xv = X[:, NI * b:NI * b + NI, :].rearrange("p i d -> p (i d)")
                st["acc", b] = do("vector", lambda e: e.tensor_tensor(xv, MI[m][:, :], xv, ALU.add),
                                  [t, st["xs", b], st.get(("acc", b))], "v_acc")
                st["mixed", b] = True
                release(m, st["acc", b])
            later(1, add)

        def load_y(b):
            st["yg", b] = dma("sync", lambda e: e.dma_start(
                xh[:, NI * b:NI * b + NI, 0:D], ys_d[b * S:b * S + S, :].rearrange("(i p) d -> p i d", p=P)),
                [st["yst", NT - 1], st["yst", NT - 2], st["scat"], st["r", b], st["xnTp", b]], f"ld_yg{b}")

        def blend(b):
            before = [st["yg", b], st["alpha"], st["xs", b], st.get(("acc", b))]
            for k in range(NI * b, NI * b + NI):
                st["acc", b] = do("vector", lambda e, k=k: e.scalar_tensor_tensor(
                    out=X[:, k, :], in0=xh[:, k, 0:D], scalar=alpha[:, k:k + 1], in1=X[:, k, :], op0=ALU.mult,
                    op1=ALU.add), before, "v_fin")

        def store(b):
            st["out", b] = dma("sync", lambda e: e.dma_start(
                out_d[b].rearrange("(i p) d -> p i d", p=P), X[:, NI * b:NI * b + NI, :]), [st["acc", b]], "st_out")

        NS, W = NB * NG, 11
        stats(0)
        invert(0, 1)
        consts = None
        for t, k in ((idb, K_ID), (trib, K_TRI), (oneb, K_ONE), (lowb, K_LOW)):
            consts = do("scalar", lambda e, t=t, k=k: e.activation(t[:, :], cst[:, k:k + P], ACT.Copy),
                        [l_c], "consts")
        norm(0)
        rope(0, "vector")
        project_in(0)
        stats(1)
        stats(2)
        project(0, "k")
        stats(3)
        project(0, "q")
        stats(4)
        project_v(0)
        router_in(0)
        router(0)
        operands(0)
        st["q"] = None
        q0 = [st["q", a] for a in range(3)]
        pads.append(load_pad(1))
        zero_x = dma("sync", lambda e: e.dma_start(xs_d, blank_d), sem="zx")
        for b in range(5, NB):
            stats(b)
        invert(1, NB)
        norm(1)
        rope(1, "gpsimd")
        norm(2)
        clock[0] = 1
        side = {}

        def at(slot, fn, *a):
            side.setdefault(slot, []).append(lambda: fn(*a))

        M0, M1 = 4, 9
        SO, PO, HO = 12, 21, 34
        RS, RD, SR, ND, GO, LST = 18, 4, 1.4, 2, 10, 11
        I1, I2 = 7, 18
        for n in range(NS):
            b, g = n // NG, n % NG
            for j, f in enumerate(max_units(n)):
                at(W * n + j, f)
            at(W * n + W - 1, max_split, n)
        for n in range(NS):
            for j, f in enumerate(score_units(n)):
                at(W * n + W + SO + j, f)
            at(W * n + W + 3, max_rows, n)
        lists = {}
        for n in range(NS):
            b, g = n // NG, n % NG
            s = W * n + W
            for j, f in enumerate(pv_units(n)):
                lists.setdefault(s + PO + 3 * j, []).append(f)
            if b < NB - 1:
                lists.setdefault(s + HO, []).append(lambda n=n: heads(n))
                if g == NG - 1:
                    lists.setdefault(s + HO + I1, []).append(lambda b=b: invert_sums(b))
                    lists.setdefault(s + HO + I2, []).append(lambda b=b: mix(b))
            else:
                lists.setdefault(s + PO + 11, []).append(lambda n=n: heads_now(n))
                if g == NG - 1:
                    lists.setdefault(s + PO + 13, []).append(lambda b=b: mix_now(b))
        core, side = side, {}
        for b in range(3, NB):
            at(ND * (b - 2), norm, b)
        for b in range(2, NB):
            at(3 if b == 2 else W * (b - 2) + 2, rope, b, "gpsimd")
        for b in range(1, NB):
            at(RS + RD * (b - 1), router_in, b)
            at(RS + RD * (b - 1) + 2, router, b)
        for b in range(NB):
            at(RS + 1 + RD * b, squares, b)
        end = RS + RD * 7 + 1
        at(end, lambda: spread(route()))
        at(end + 2, invert2)
        for t in range(3):
            at(end + 14, weights, t)
        for k in range(NK):
            at(end + 16 + int(k * SR), scatter, k)
        end += 16 + int(NK * SR)
        for t in range(3):
            at(end + 1, load_tile, t)
        at(end + GO - 4, ffn_norm, 0)
        for k in range(NK):
            at(2 * W + W * k, residual, k)
        for b in range(1, NB):
            s = W * (2 if b == 1 else 4 * b - 4)
            at(s + 1, project_in, b)
            at(s + 3, project, b, "k")
            at(s + 5, project, b, "q")
            at(s + 7, project_v, b)
            at(34 if b == 1 else W * (4 * b - 2) + 2, operands, b)
        todo = []
        for t in range(NT + 1):
            if t < NT:
                todo.append(lambda t=t: (ffn_in(t), ffn_norm(t + 1) if t + 1 < NT else None))
            if t > 0:
                todo.append(lambda t=t: ffn_down(t - 1, 0))
                todo.append(lambda t=t: ffn_down(t - 1, 1))
            if t < NT:
                todo.append(lambda t=t: ffn_up(t, 0))
                todo.append(lambda t=t: ffn_up(t, 1))
            if t > 0:
                todo.append(lambda t=t: ffn_out(t - 1))
        todo.append(lambda: [load_y(b) for b in range(NB)])
        first, last = end + GO, W * NS + LST
        ffn = {}
        for i, f in enumerate(todo):
            ffn.setdefault(first + (last - first) * i // len(todo), []).append(f)
        slot = blended = 0
        while slot <= max(max(lists), last) or pending or blended < NB:
            tick()
            for d in (core, side, ffn, lists):
                for f in d.get(slot, []):
                    f()
            slot += 1
            if slot > last + 8 and blended < NB:
                blend(blended)
                blended += 1
            for b in range(blended):
                if ("mixed", b) in st and ("out", b) not in st:
                    store(b)
        fl.wait("sync", [st["out", NB - 1], st["yst", NT - 1], st["yst", NT - 2], st["scat"], zero_x,
                         st["q"], st["k"]])
        fl.run(ctx.enter_context(nc.Block()))


def kernel(**inputs):
    import concourse.bacc as bacc
    from concourse.bass_utils import run_bass_kernel_spmd

    a = {k[3:]: np.asarray(v) for k, v in inputs.items()}
    f32 = np.float32
    tab = np.zeros((E, P, ROW), f32)
    tab[:, :, C_W1:C_W1 + F] = a["ffn_W1"].transpose(0, 2, 1)
    tab[:, :, C_W2:C_W2 + F] = a["ffn_W2"].transpose(0, 2, 1).reshape(E, 4, P, D).transpose(0, 2, 1, 3).reshape(E, P, F)
    tab[:, :, C_G] = a["ffn_gamma"]
    tab[:, :, C_B] = a["ffn_beta"]
    tab[:, :, C_B1:C_B1 + 4] = a["ffn_b1"].reshape(E, 4, P).transpose(0, 2, 1)
    tab[:, :, C_B2:C_B2 + D] = a["ffn_b2"][:, None, :]
    cst = np.zeros((P, KW), f32)
    p = np.arange(P)
    cst[:, K_ID:K_ID + P] = np.eye(P)
    cst[:, K_MASK + S - P:K_MASK + S] = np.where(p[None, :] > p[:, None], -1e30, 0.0)
    cst[:, K_LOW:K_LOW + P] = np.where(p[None, :] < p[:, None], -1e30, 0.0)
    cst[:, K_TRI:K_TRI + P] = p[:, None] < p[None, :]
    cst[:, K_ONE:K_ONE + P] = 1.0
    theta = (f32(1.0) / f32(10000.0) ** (np.arange(64, dtype=f32) / f32(64))).astype(f32)
    ang = np.arange(S, dtype=f32)[:, None] * theta[None, :]
    for k, fn in ((K_COS, np.cos), (K_SIN, np.sin)):
        cst[:, k:k + 256] = fn(ang).astype(f32).reshape(NI, P, 64).transpose(1, 0, 2).reshape(P, 256)
    cst[:, K_IE:K_IE + E] = np.arange(E)
    cst[:, K_IE8:K_IE8 + E] = np.arange(E) + 8
    cst[:, K_J:K_J + 32] = np.arange(32) * P
    cst[:, K_T:K_T + NT] = np.arange(NT)
    cst[:, K_P] = p
    cst[:, K_TOK:K_TOK + NK] = np.arange(NK)[None, :] * P + p[:, None]
    pad = np.zeros((P - 72, 5120), f32)
    pad[MROW - 72:MROW - 70, 0:1024].view(np.uint32)[:] = 0x3F803F80
    blank = np.zeros((NT * P, XW), f32)
    blank[:, C_TOK] = NK * P + np.arange(NT * P)
    arrays = {
        "X": a["attn_X"],
        "wq": a["attn_W_q"].reshape(NH, 8, D).transpose(2, 1, 0).reshape(D, P),
        "wkv": np.concatenate([a["attn_W_k"].reshape(NG, 8, D).transpose(2, 1, 0).reshape(D, 32),
                               a["attn_W_v"].T], axis=1),
        "wo": a["attn_W_o"].T,
        "cen": a["ffn_centroids"].T,
        "tab": tab.reshape(E * P, ROW),
        "cst": cst,
        "pad": pad,
        "blank": blank,
    }
    arrays = {"in_" + k: np.ascontiguousarray(v) for k, v in arrays.items()}
    nc = bacc.Bacc("TRN2", target_bir_lowering=False, num_devices=1)
    args = [nc.dram_tensor(k, v.shape, mybir.dt.from_np(v.dtype), kind="ExternalInput").ap() for k, v in arrays.items()]
    out = nc.dram_tensor("out", (NB, S, D), F32, kind="ExternalOutput").ap()
    build(nc, *args, out)
    r = run_bass_kernel_spmd(nc, [arrays], core_ids=[0])
    return r.results[0]["out"]
```
